# Optimizing a Trainium2 kernel written in Bass

```python
import numpy as np
import jax
import jax.numpy as jnp

def _softmax(x, axis=-1):
    return jax.nn.softmax(x, axis=axis)

def _gelu(x):
    return jax.nn.gelu(x, approximate=True)

def _silu(x):
    return jax.nn.silu(x)

def _sigmoid(x):
    return jax.nn.sigmoid(x)

def _layernorm(x, axis=-1, eps=1e-05):
    m = jnp.mean(x, axis=axis, keepdims=True)
    v = jnp.var(x, axis=axis, keepdims=True)
    return (x - m) / jnp.sqrt(v + eps)

def _scatter_add(tgt, idx, src, axis=0):
    return tgt.at[idx].add(src)

def _segment_sum(src, seg, n):
    return jax.ops.segment_sum(src, seg, n)
kernel_name = 'mk_xattn_ffn_d2_seqx_r8_8adbdd'

def setup_inputs(seed: int=0):
    np.random.seed(seed)
    _w = jnp.asarray

    def _rec_inputs():
        import jax
        import jax.numpy as jnp
        _rk = jax.random.key(seed)
        x = -0.0002928 + 1 * jax.random.normal(jax.random.fold_in(_rk, 1), (4, 256, 128), jnp.float32)
        _lenS = 256 - jax.random.randint(jax.random.fold_in(_rk, 7), (4,), 0, max(1, 256 // 4) + 1, jnp.int32)
        _lenS2 = 512 - jax.random.randint(jax.random.fold_in(_rk, 8), (4,), 0, max(1, 512 // 4) + 1, jnp.int32)
        _ctx_1024P = jax.random.normal(jax.random.fold_in(_rk, 11), (4, 16, 128), jnp.float32)
        _ctx_1024c = jax.random.dirichlet(jax.random.fold_in(_rk, 511), 0.3 * jnp.ones((16,), jnp.float32), (4, 512))
        _ctx_1024t = jnp.einsum('bsk,bkd->bsd', _ctx_1024c, _ctx_1024P)
        _ctx_1024t = _ctx_1024t * jax.lax.rsqrt(jnp.mean(jnp.square(_ctx_1024t)) + 1e-12) * 0.953939
        ctx_1024 = -0.000191848 + 0.999787 * (_ctx_1024t + 0.3 * jax.random.normal(jax.random.fold_in(_rk, 611), (4, 512, 128), jnp.float32))
        _validS = jnp.arange(256)[None, :] < _lenS[:, None]
        _validS2 = jnp.arange(512)[None, :] < _lenS2[:, None]
        _causal = jnp.tril(jnp.ones((256, 256), dtype=bool))
        mask_BxS2_bk0 = jnp.logical_not(jnp.broadcast_to(_validS2[:, :], (4, 512)))
        mask_BxSxS2_bk1 = jnp.broadcast_to(_validS2[:, None, :], (4, 256, 512))
        return (x, ctx_1024, mask_BxS2_bk0, mask_BxSxS2_bk1)
    x, ctx_1024, mask_BxS2_bk0, mask_BxSxS2_bk1 = _rec_inputs()

    def _L0_xattn_setup():
        import jax, jax.numpy as jnp
        import numpy as np
        NUM_HEADS = 16
        EPS = 1e-06

        def _ln(t, w, b):
            mu = jnp.mean(t, axis=-1, keepdims=True)
            var = jnp.mean(jnp.square(t - mu), axis=-1, keepdims=True)
            return (t - mu) * jax.lax.rsqrt(var + EPS) * w + b
        key = jax.random.key(seed)
        ks = jax.random.split(key, 10)
        b, s1, s2, qdim, kdim = (2, 256, 384, 128, 128)
        d = qdim // NUM_HEADS
        x = jax.random.normal(ks[0], (b, s1, qdim), dtype=jnp.float32)
        y = jax.random.normal(ks[1], (b, s2, kdim), dtype=jnp.float32)
        padding_mask = jax.random.randint(ks[2], (b, s2), 0, 2) > 0
        padding_mask = padding_mask.at[:, 0].set(True)
        w = 0.02
        Wq = jax.random.normal(ks[3], (qdim, qdim), dtype=jnp.float32) * w
        bq = jnp.zeros((qdim,), jnp.float32)
        Wkv = jax.random.normal(ks[4], (2 * qdim, kdim), dtype=jnp.float32) * w
        bkv = jnp.zeros((2 * qdim,), jnp.float32)
        qn_w = jnp.ones((d,), jnp.float32)
        qn_b = jnp.zeros((d,), jnp.float32)
        kn_w = jnp.ones((d,), jnp.float32)
        kn_b = jnp.zeros((d,), jnp.float32)
        Wo = jax.random.normal(ks[5], (qdim, qdim), dtype=jnp.float32) * w
        bo = jnp.zeros((qdim,), jnp.float32)
        return {'x': x, 'y': y, 'padding_mask': padding_mask, 'Wq': Wq, 'bq': bq, 'Wkv': Wkv, 'bkv': bkv, 'qn_w': qn_w, 'qn_b': qn_b, 'kn_w': kn_w, 'kn_b': kn_b, 'Wo': Wo, 'bo': bo}
    _L0_xattn_all = _L0_xattn_setup()
    _L0_xattn_in = {k: v for k, v in _L0_xattn_all.items() if k in ('Wq', 'bq', 'Wkv', 'bkv', 'qn_w', 'qn_b', 'kn_w', 'kn_b', 'Wo', 'bo')}
    del _L0_xattn_all

    def _L0_ffn_setup():
        import jax, jax.numpy as jnp
        import numpy as np
        D_MODEL = 128
        NHEAD = 16
        HEAD_DIM = D_MODEL // NHEAD
        FF = 256
        NUM_EXPERTS = 8
        EPS = 1e-05

        def _ln(x, g, b):
            m = x.mean(-1, keepdims=True)
            v = ((x - m) ** 2).mean(-1, keepdims=True)
            return (x - m) / jnp.sqrt(v + EPS) * g + b

        def _attention(src, Wq, bq, Wk, bk, Wv, bv, Wo, bo):
            B, T, d = src.shape
            scale = HEAD_DIM ** (-0.5)
            q = (src @ Wq + bq).reshape(B, T, NHEAD, HEAD_DIM)
            k = (src @ Wk + bk).reshape(B, T, NHEAD, HEAD_DIM)
            v = (src @ Wv + bv).reshape(B, T, NHEAD, HEAD_DIM)
            scores = jnp.einsum('bqhd,bkhd->bhqk', q, k) * scale
            probs = jax.nn.softmax(scores, axis=-1)
            out = jnp.einsum('bhqk,bkhd->bqhd', probs, v).reshape(B, T, d)
            return out @ Wo + bo

        def _moe(x, gW, gb, W1, b1, W2, b2):
            B, T, d = x.shape
            xf = x.reshape(-1, d)
            gates = jax.nn.softmax(xf @ gW + gb, axis=-1)
            top2_scores, top2_idx = jax.lax.top_k(gates, 2)
            w = (jax.nn.one_hot(top2_idx, NUM_EXPERTS, dtype=xf.dtype) * top2_scores[..., None]).sum(1)
            h = jax.nn.relu(jnp.einsum('nd,edf->enf', xf, W1) + b1[:, None, :])
            y = jnp.einsum('enf,efd->end', h, W2) + b2[:, None, :]
            out = jnp.einsum('ne,end->nd', w, y)
            return out.reshape(B, T, d)
        key = jax.random.key(seed)
        ks = jax.random.split(key, 12)
        s = 0.02
        d, f, E = (D_MODEL, FF, NUM_EXPERTS)
        return {'src': jax.random.normal(ks[0], (8, 64, d), dtype=jnp.float32), 'Wq': jax.random.normal(ks[1], (d, d), dtype=jnp.float32) * s, 'bq': jnp.zeros((d,), jnp.float32), 'Wk': jax.random.normal(ks[2], (d, d), dtype=jnp.float32) * s, 'bk': jnp.zeros((d,), jnp.float32), 'Wv': jax.random.normal(ks[3], (d, d), dtype=jnp.float32) * s, 'bv': jnp.zeros((d,), jnp.float32), 'Wo': jax.random.normal(ks[4], (d, d), dtype=jnp.float32) * s, 'bo': jnp.zeros((d,), jnp.float32), 'gW': jax.random.normal(ks[5], (d, E), dtype=jnp.float32) * s, 'gb': jnp.zeros((E,), jnp.float32), 'W1': jax.random.normal(ks[6], (E, d, f), dtype=jnp.float32) * s, 'b1': jnp.zeros((E, f), jnp.float32), 'W2': jax.random.normal(ks[7], (E, f, d), dtype=jnp.float32) * s, 'b2': jnp.zeros((E, d), jnp.float32), 'ln1_g': jnp.ones((d,), jnp.float32), 'ln1_b': jnp.zeros((d,), jnp.float32), 'ln2_g': jnp.ones((d,), jnp.float32), 'ln2_b': jnp.zeros((d,), jnp.float32)}
    _L0_ffn_all = _L0_ffn_setup()
    _L0_ffn_in = {k: v for k, v in _L0_ffn_all.items() if k in ('Wq', 'bq', 'Wk', 'bk', 'Wv', 'bv', 'Wo', 'bo', 'gW', 'gb', 'W1', 'b1', 'W2', 'b2', 'ln1_g', 'ln1_b', 'ln2_g', 'ln2_b')}
    del _L0_ffn_all

    def _L1_xattn_setup():
        import jax, jax.numpy as jnp
        import numpy as np
        B, S, T = (4, 256, 256)
        D_Q = D_C = D_OUT = 128
        HEADS = 16
        HW = D_Q // HEADS
        MASK_FILL = -100000000.0
        rng = jax.random.key(seed)
        ks = jax.random.split(rng, 12)
        inp = {'query': jax.random.normal(ks[0], (B, S, D_Q), dtype=jnp.float32), 'key': jax.random.normal(ks[1], (B, T, D_C), dtype=jnp.float32), 'value': jax.random.normal(ks[2], (B, T, D_C), dtype=jnp.float32), 'mask': jax.random.randint(ks[3], (B, S, T), 0, 2).astype(bool), 'Wq': jax.random.normal(ks[4], (D_Q, HEADS, HW), dtype=jnp.float32) * 0.02, 'bq': jax.random.normal(ks[5], (HEADS, HW), dtype=jnp.float32) * 0.02, 'Wk': jax.random.normal(ks[6], (D_C, HEADS, HW), dtype=jnp.float32) * 0.02, 'bk': jax.random.normal(ks[7], (HEADS, HW), dtype=jnp.float32) * 0.02, 'Wv': jax.random.normal(ks[8], (D_C, HEADS, HW), dtype=jnp.float32) * 0.02, 'bv': jax.random.normal(ks[9], (HEADS, HW), dtype=jnp.float32) * 0.02, 'Wo': jax.random.normal(ks[10], (HEADS, HW, D_OUT), dtype=jnp.float32) * 0.02, 'bo': jax.random.normal(ks[11], (D_OUT,), dtype=jnp.float32) * 0.02}
        return inp
    _L1_xattn_all = _L1_xattn_setup()
    _L1_xattn_in = {k: v for k, v in _L1_xattn_all.items() if k in ('Wq', 'bq', 'Wk', 'bk', 'Wv', 'bv', 'Wo', 'bo')}
    del _L1_xattn_all

    def _L1_ffn_setup():
        import jax, jax.numpy as jnp
        import numpy as np
        B, T, C = (4, 256, 128)
        H, E = (512, 8)
        key = jax.random.key(seed)
        ks = jax.random.split(key, 6)
        scale = 0.02
        x = jax.random.normal(ks[0], (B, T, C), dtype=jnp.float32)
        w_router = jax.random.normal(ks[1], (C, E), dtype=jnp.float32) * scale
        b_router = jnp.zeros((E,), dtype=jnp.float32)
        w1 = jax.random.normal(ks[2], (E, C, H), dtype=jnp.float32) * scale
        b1 = jnp.zeros((E, H), dtype=jnp.float32)
        w2 = jax.random.normal(ks[3], (E, H, C), dtype=jnp.float32) * scale
        b2 = jnp.zeros((E, C), dtype=jnp.float32)
        return {'x': x, 'w_router': w_router, 'b_router': b_router, 'w1': w1, 'b1': b1, 'w2': w2, 'b2': b2}
    _L1_ffn_all = _L1_ffn_setup()
    _L1_ffn_in = {k: v for k, v in _L1_ffn_all.items() if k in ('w_router', 'b_router', 'w1', 'b1', 'w2', 'b2')}
    del _L1_ffn_all
    return {'x': x, 'ctx_1024': ctx_1024, 'mask_BxS2_bk0': mask_BxS2_bk0, 'mask_BxSxS2_bk1': mask_BxSxS2_bk1, 'L0_xattn_Wq': _L0_xattn_in['Wq'], 'L0_xattn_bq': _L0_xattn_in['bq'], 'L0_xattn_Wkv': _L0_xattn_in['Wkv'], 'L0_xattn_bkv': _L0_xattn_in['bkv'], 'L0_xattn_qn_w': _L0_xattn_in['qn_w'], 'L0_xattn_qn_b': _L0_xattn_in['qn_b'], 'L0_xattn_kn_w': _L0_xattn_in['kn_w'], 'L0_xattn_kn_b': _L0_xattn_in['kn_b'], 'L0_xattn_Wo': _L0_xattn_in['Wo'], 'L0_xattn_bo': _L0_xattn_in['bo'], 'L0_ffn_Wq': _L0_ffn_in['Wq'], 'L0_ffn_bq': _L0_ffn_in['bq'], 'L0_ffn_Wk': _L0_ffn_in['Wk'], 'L0_ffn_bk': _L0_ffn_in['bk'], 'L0_ffn_Wv': _L0_ffn_in['Wv'], 'L0_ffn_bv': _L0_ffn_in['bv'], 'L0_ffn_Wo': _L0_ffn_in['Wo'], 'L0_ffn_bo': _L0_ffn_in['bo'], 'L0_ffn_gW': _L0_ffn_in['gW'], 'L0_ffn_gb': _L0_ffn_in['gb'], 'L0_ffn_W1': _L0_ffn_in['W1'], 'L0_ffn_b1': _L0_ffn_in['b1'], 'L0_ffn_W2': _L0_ffn_in['W2'], 'L0_ffn_b2': _L0_ffn_in['b2'], 'L0_ffn_ln1_g': _L0_ffn_in['ln1_g'], 'L0_ffn_ln1_b': _L0_ffn_in['ln1_b'], 'L0_ffn_ln2_g': _L0_ffn_in['ln2_g'], 'L0_ffn_ln2_b': _L0_ffn_in['ln2_b'], 'L1_xattn_Wq': _L1_xattn_in['Wq'], 'L1_xattn_bq': _L1_xattn_in['bq'], 'L1_xattn_Wk': _L1_xattn_in['Wk'], 'L1_xattn_bk': _L1_xattn_in['bk'], 'L1_xattn_Wv': _L1_xattn_in['Wv'], 'L1_xattn_bv': _L1_xattn_in['bv'], 'L1_xattn_Wo': _L1_xattn_in['Wo'], 'L1_xattn_bo': _L1_xattn_in['bo'], 'L1_ffn_w_router': _L1_ffn_in['w_router'], 'L1_ffn_b_router': _L1_ffn_in['b_router'], 'L1_ffn_w1': _L1_ffn_in['w1'], 'L1_ffn_b1': _L1_ffn_in['b1'], 'L1_ffn_w2': _L1_ffn_in['w2'], 'L1_ffn_b2': _L1_ffn_in['b2']}

def reference(x, ctx_1024, mask_BxS2_bk0, mask_BxSxS2_bk1, L0_xattn_Wq, L0_xattn_bq, L0_xattn_Wkv, L0_xattn_bkv, L0_xattn_qn_w, L0_xattn_qn_b, L0_xattn_kn_w, L0_xattn_kn_b, L0_xattn_Wo, L0_xattn_bo, L0_ffn_Wq, L0_ffn_bq, L0_ffn_Wk, L0_ffn_bk, L0_ffn_Wv, L0_ffn_bv, L0_ffn_Wo, L0_ffn_bo, L0_ffn_gW, L0_ffn_gb, L0_ffn_W1, L0_ffn_b1, L0_ffn_W2, L0_ffn_b2, L0_ffn_ln1_g, L0_ffn_ln1_b, L0_ffn_ln2_g, L0_ffn_ln2_b, L1_xattn_Wq, L1_xattn_bq, L1_xattn_Wk, L1_xattn_bk, L1_xattn_Wv, L1_xattn_bv, L1_xattn_Wo, L1_xattn_bo, L1_ffn_w_router, L1_ffn_b_router, L1_ffn_w1, L1_ffn_b1, L1_ffn_w2, L1_ffn_b2):
    import jax
    import jax.numpy as jnp

    def _L0_xattn_ref(x, y, padding_mask, Wq, bq, Wkv, bkv, qn_w, qn_b, kn_w, kn_b, Wo, bo):
        import jax, jax.numpy as jnp
        import numpy as np
        NUM_HEADS = 16
        EPS = 1e-06

        def _ln(t, w, b):
            mu = jnp.mean(t, axis=-1, keepdims=True)
            var = jnp.mean(jnp.square(t - mu), axis=-1, keepdims=True)
            return (t - mu) * jax.lax.rsqrt(var + EPS) * w + b
        b, s1, c = x.shape
        s2 = y.shape[1]
        h, d = (NUM_HEADS, c // NUM_HEADS)
        scale = d ** (-0.5)
        q = (x @ Wq.T + bq).reshape(b, s1, h, d)
        kv = (y @ Wkv.T + bkv).reshape(b, s2, 2, h, d)
        k, v = (kv[:, :, 0], kv[:, :, 1])
        q = _ln(q, qn_w, qn_b) * scale
        k = _ln(k, kn_w, kn_b)
        attn = jnp.einsum('bihd,bjhd->bhij', q, k)
        attn = jnp.where(padding_mask[:, None, None, :], attn, -jnp.inf)
        p = jax.nn.softmax(attn, axis=-1)
        ctx = jnp.einsum('bhij,bjhd->bihd', p, v).reshape(b, s1, c)
        out = ctx @ Wo.T + bo
        return out

    def _L0_ffn_ref(src, Wq, bq, Wk, bk, Wv, bv, Wo, bo, gW, gb, W1, b1, W2, b2, ln1_g, ln1_b, ln2_g, ln2_b):
        import jax, jax.numpy as jnp
        import numpy as np
        D_MODEL = 128
        NHEAD = 16
        HEAD_DIM = D_MODEL // NHEAD
        FF = 256
        NUM_EXPERTS = 8
        EPS = 1e-05

        def _ln(x, g, b):
            m = x.mean(-1, keepdims=True)
            v = ((x - m) ** 2).mean(-1, keepdims=True)
            return (x - m) / jnp.sqrt(v + EPS) * g + b

        def _attention(src, Wq, bq, Wk, bk, Wv, bv, Wo, bo):
            B, T, d = src.shape
            scale = HEAD_DIM ** (-0.5)
            q = (src @ Wq + bq).reshape(B, T, NHEAD, HEAD_DIM)
            k = (src @ Wk + bk).reshape(B, T, NHEAD, HEAD_DIM)
            v = (src @ Wv + bv).reshape(B, T, NHEAD, HEAD_DIM)
            scores = jnp.einsum('bqhd,bkhd->bhqk', q, k) * scale
            probs = jax.nn.softmax(scores, axis=-1)
            out = jnp.einsum('bhqk,bkhd->bqhd', probs, v).reshape(B, T, d)
            return out @ Wo + bo

        def _moe(x, gW, gb, W1, b1, W2, b2):
            B, T, d = x.shape
            xf = x.reshape(-1, d)
            gates = jax.nn.softmax(xf @ gW + gb, axis=-1)
            top2_scores, top2_idx = jax.lax.top_k(gates, 2)
            w = (jax.nn.one_hot(top2_idx, NUM_EXPERTS, dtype=xf.dtype) * top2_scores[..., None]).sum(1)
            h = jax.nn.relu(jnp.einsum('nd,edf->enf', xf, W1) + b1[:, None, :])
            y = jnp.einsum('enf,efd->end', h, W2) + b2[:, None, :]
            out = jnp.einsum('ne,end->nd', w, y)
            return out.reshape(B, T, d)
        attn_out = _attention(src, Wq, bq, Wk, bk, Wv, bv, Wo, bo)
        x = _ln(src + attn_out, ln1_g, ln1_b)
        ff = _moe(x, gW, gb, W1, b1, W2, b2)
        return _ln(x + ff, ln2_g, ln2_b)

    def _L1_xattn_ref(query, key, value, mask, Wq, bq, Wk, bk, Wv, bv, Wo, bo):
        import jax, jax.numpy as jnp
        import numpy as np
        B, S, T = (4, 256, 256)
        D_Q = D_C = D_OUT = 128
        HEADS = 16
        HW = D_Q // HEADS
        MASK_FILL = -100000000.0
        q = jnp.einsum('bse,ehd->bhsd', query, Wq) + bq[:, None, :]
        k = jnp.einsum('bte,ehd->bhtd', key, Wk) + bk[:, None, :]
        v = jnp.einsum('bte,ehd->bhtd', value, Wv) + bv[:, None, :]
        logits = jnp.einsum('bhsd,bhtd->bhst', q, k)
        logits = jnp.where(mask[:, None, :, :], MASK_FILL, logits)
        score = jax.nn.softmax(logits, axis=-1)
        attn = jnp.einsum('bhst,bhtd->bhsd', score, v)
        attn = attn / jnp.sqrt(jnp.float32(HW))
        out = jnp.einsum('bhsd,hdo->bso', attn, Wo) + bo
        return out

    def _L1_ffn_ref(x, w_router, b_router, w1, b1, w2, b2):
        import jax, jax.numpy as jnp
        import numpy as np
        B, T, C = (4, 256, 128)
        H, E = (512, 8)
        logits = jnp.einsum('btc,ce->bte', x, w_router) + b_router
        probs = jax.nn.softmax(logits, axis=-1)
        top1 = jnp.argmax(probs, axis=-1)
        out = jnp.zeros_like(x)
        for e in range(E):
            h = jax.nn.gelu(jnp.einsum('btc,ch->bth', x, w1[e]) + b1[e], approximate=False)
            y = jnp.einsum('bth,hc->btc', h, w2[e]) + b2[e]
            out = out + jnp.where((top1 == e)[..., None], y, 0.0)
        return out
    x = x + _L0_xattn_ref(_layernorm(x, axis=-1), ctx_1024, mask_BxS2_bk0, L0_xattn_Wq, L0_xattn_bq, L0_xattn_Wkv, L0_xattn_bkv, L0_xattn_qn_w, L0_xattn_qn_b, L0_xattn_kn_w, L0_xattn_kn_b, L0_xattn_Wo, L0_xattn_bo)
    x = x + _L0_ffn_ref(_layernorm(x, axis=-1), L0_ffn_Wq, L0_ffn_bq, L0_ffn_Wk, L0_ffn_bk, L0_ffn_Wv, L0_ffn_bv, L0_ffn_Wo, L0_ffn_bo, L0_ffn_gW, L0_ffn_gb, L0_ffn_W1, L0_ffn_b1, L0_ffn_W2, L0_ffn_b2, L0_ffn_ln1_g, L0_ffn_ln1_b, L0_ffn_ln2_g, L0_ffn_ln2_b)
    x = x + _L1_xattn_ref(_layernorm(x, axis=-1), ctx_1024, ctx_1024, mask_BxSxS2_bk1, L1_xattn_Wq, L1_xattn_bq, L1_xattn_Wk, L1_xattn_bk, L1_xattn_Wv, L1_xattn_bv, L1_xattn_Wo, L1_xattn_bo)
    x = x + _L1_ffn_ref(_layernorm(x, axis=-1), L1_ffn_w_router, L1_ffn_b_router, L1_ffn_w1, L1_ffn_b1, L1_ffn_w2, L1_ffn_b2)
    return x

_drawn_inputs = setup_inputs


def setup_inputs(seed=0):
    import zlib

    import numpy as np

    out = dict(_drawn_inputs(seed))
    spreads = {'L0_xattn_bq': (0.0, 0.8),
     'L0_xattn_bkv': (0.0, 0.359),
     'L0_xattn_qn_w': (1.0, 0.6),
     'L0_xattn_qn_b': (0.0, 0.8),
     'L0_xattn_kn_w': (1.0, 0.6),
     'L0_xattn_kn_b': (0.0, 0.8),
     'L0_xattn_bo': (0.0, 0.1),
     'L0_ffn_bq': (0.0, 0.8),
     'L0_ffn_bk': (0.0, 0.8),
     'L0_ffn_bv': (0.0, 0.616),
     'L0_ffn_bo': (0.0, 0.1),
     'L0_ffn_gb': (0.0, 0.8),
     'L0_ffn_b1': (0.0, 0.8),
     'L0_ffn_b2': (0.0, 0.627),
     'L0_ffn_ln1_g': (1.0, 0.2),
     'L0_ffn_ln1_b': (0.0, 0.1),
     'L0_ffn_ln2_g': (1.0, 0.2),
     'L0_ffn_ln2_b': (0.0, 0.1),
     'L1_ffn_b_router': (0.0, 0.1),
     'L1_ffn_b1': (0.0, 0.675),
     'L1_ffn_b2': (0.0, 0.1)}
    factors = {'L0_xattn_Wq': 5.045,
     'L0_ffn_Wq': 8.0,
     'L0_ffn_Wk': 8.0,
     'L0_ffn_Wv': 8.0,
     'L0_ffn_Wo': 4.343,
     'L0_ffn_gW': 4.86,
     'L0_ffn_W1': 7.965,
     'L0_ffn_W2': 7.103,
     'L1_xattn_Wq': 8.0,
     'L1_xattn_bq': 8.0,
     'L1_xattn_Wk': 8.0,
     'L1_xattn_bk': 8.0,
     'L1_xattn_Wv': 8.0,
     'L1_xattn_bv': 8.0,
     'L1_xattn_Wo': 8.0,
     'L1_xattn_bo': 4.226}
    for name, (base, spread) in spreads.items():
        noise = np.random.default_rng([zlib.crc32(name.encode()), seed]).standard_normal(out[name].shape)
        drawn = base * np.exp(spread * noise) if base else spread * noise
        out[name] = jnp.asarray(drawn.astype(out[name].dtype))
    for name, factor in factors.items():
        out[name] = (out[name] * factor).astype(out[name].dtype)
    return out
```

```python
import concourse.bass as bass
from concourse import mybir
from contextlib import ExitStack

F32 = mybir.dt.float32
BF16 = mybir.dt.bfloat16
U8 = mybir.dt.uint8
U32 = mybir.dt.uint32
ALU = mybir.AluOpType
ACT = mybir.ActivationFunctionType
AX = mybir.AxisListType

P = 128
B, SQ, SK, D = 4, 256, 512, 128
H, DH = 16, 8
TOK = B * SQ
NT = TOK // P
HU = 4
UPB = H // HU
UNITS = B * UPB
LEAD = 3
QT = SQ // P
E = 8
CH = 512
QPART = (0, 0, 0, 1, 1, 2)
KPART = (0, 1, 2, 0, 1, 0)
K_RUNS = ((0, 3), (3, 2), (5, 1))
ROW_MASK, ROW_MAX = 64, 96
KROWS = ROW_MAX + 1
VW = 32
MASKED = -(2.0 ** 99)
LOWEST = -3.0e38
ONES_PAIR = 1.0019378662109375
MINUS_ONES_PAIR = -1.0058441162109375
ISQ = DH ** -0.5


class Phase:

    def __init__(self, name, nk, sem, qk_norm, mask):
        self.name, self.nk, self.qk_norm, self.mask = name, nk, qk_norm, mask
        self.kw = nk * P
        kc = B * self.kw // CH
        jobs = []
        for c in range(kc):
            jobs.append(("k", c))
            if c < TOK // CH:
                jobs.append(("q", c))
        self.jobs = jobs
        self.vt = B * nk
        s = lambda what: sem(f"{name}_{what}")
        self.w_loaded = s("w_loaded")
        self.proj_ready = s("proj_ready")
        self.u_ready = qk_norm and s("u_ready")
        self.cent_ready = qk_norm and s("cent_ready")
        self.sq_ready = qk_norm and s("sq_ready")
        self.var_ready = qk_norm and s("var_ready")
        self.sd_ready = qk_norm and s("sd_ready")
        self.full_ready = s("full_ready")
        self.hi_ready = s("hi_ready")
        self.rest_ready = s("rest_ready")
        self.mid_ready = s("mid_ready")
        self.parts_ready = s("parts_ready")
        self.kept = [s(f"kept{r}") for r in range(2)]
        self.placed = s("placed")
        self.maskrow_placed = mask != "full" and s("maskrow_placed")
        self.v_ps = s("v_ps")
        self.v_ready = s("v_ready")
        self.v_masked = mask == "key" and s("v_masked")
        self.vcur_ready = s("vcur_ready")
        self.mcur_ready = mask == "full" and s("mcur_ready")
        self.max_ps = s("max_ps")
        self.max_done = s("max_done")
        self.max_half = mask == "full" and s("max_half")
        self.max_col = mask == "full" and s("max_col")
        self.max_row = s("max_row")
        self.max_placed = [s(f"max_placed{r}") for r in range(2)]
        self.st_ps = s("st_ps")
        self.exp_done = s("exp_done")
        self.pv_done = s("pv_done")
        self.o_ready = s("o_ready")
        self.ot_ps = s("ot_ps")
        self.rd_ready = s("rd_ready")
        self.norm_done = s("norm_done")
        self.att_ps = s("att_ps")
        self.att_ready = s("att_ready")
        self.out_ps = s("out_ps")
        self.out_done = s("out_done")


def batches(a, j):
    kind, c = a.jobs[j]
    w = a.kw if kind == "k" else SQ
    return range(c * CH // w, (c + 1) * CH // w), w


def kept_total(a, j):
    return sum(16 * len(batches(a, i)[0]) for i in range(j % 2, j + 1, 2))


def placed_total(a):
    return sum(16 * len(batches(a, j)[0]) * len(K_RUNS if a.jobs[j][0] == "k" else QPART)
               for j in range(len(a.jobs)))


class NormSemaphores:

    def __init__(self, sem):
        self.var_ready = sem("norm_var_ready")
        self.sd_ready = sem("norm_sd_ready")
        self.done = sem("norm_done")
        self.t_ps = sem("norm_t_ps")
        self.t_ready = sem("norm_t_ready")


class Norm:

    def __init__(self, i, halves_before, tiles_before, shared):
        self.i, self.half0, self.tile0 = i, halves_before, tiles_before
        self.var_ready, self.sd_ready, self.done = shared.var_ready, shared.sd_ready, shared.done
        self.t_ps, self.t_ready = shared.t_ps, shared.t_ready


class GateSemaphores:

    def __init__(self, sem):
        self.logit_ps = sem("gate_logit_ps")
        self.shifted = sem("gate_shifted")
        self.gate_exp = sem("gate_exp")
        self.weight_ready = sem("gate_weight_ready")
        self.wt_ps = sem("gate_wt_ps")
        self.wt_ready = sem("gate_wt_ready")
        self.b2_ps = sem("gate_b2_ps")
        self.acc_ready = sem("gate_acc_ready")


class Moe:

    def __init__(self, i, ft, sem, gates, act, topk):
        self.i, self.ft, self.act, self.topk, self.gates = i, ft, act, topk, gates
        s = lambda what: sem(f"moe{i}_{what}")
        self.small_loaded = s("small_loaded")
        self.w_loaded = [s(f"w_loaded{r}") for r in range(2)]
        self.up_ps = s("up_ps")
        self.hid_ready = s("hid_ready")
        self.down_ps = s("down_ps")
        self.down_done = s("down_done")


def build(nc, I, out):
    ctx = ExitStack()
    with ctx:
        sb = lambda name, shape, dt=F32: ctx.enter_context(nc.sbuf_tensor(name, shape, dt))
        sem = lambda name: ctx.enter_context(nc.semaphore(name))

        PS = ctx.enter_context(nc.psum_tensor("PS", [P, 8, CH], F32))
        Kop = sb("Kop", [P, B * H, SK], BF16)
        Qop = sb("Qop", [P, B * H, SQ], BF16)
        Kself = Kop[:].rearrange("p a (c k) -> p (a c) k", k=SQ)[:, 0:B * H, :]
        scratch = sb("scratch", [P, 16 * CH])
        X = sb("X", [P, NT, D])
        XN = sb("XN", [P, NT, D])
        XB = sb("XB", [P, NT, D])
        xT = sb("xT", [P, TOK])
        ctxT = sb("ctxT", [P, B * SK])
        att = sb("att", [P, B, QT, D])
        parts = sb("parts", [P, 2, 3, CH], BF16)
        Vall = sb("Vall", [P, B * H, 4, DH + 1])
        Vcur = sb("Vcur", [P, 2, 4, HU, VW])
        mqk = sb("mqk", [P, B * QT, SK], BF16)
        mkq = sb("mkq", [P, B * 2, 2 * SQ], BF16)
        osb = sb("osb", [P, 2, SQ])
        mcur = sb("mcur", [P, 2, QT, SK], BF16)
        junk = parts[:].rearrange("p r s c -> p (r s) c")
        mstf = sb("mstf", [P, 2, 32])
        gate = sb("gate", [P, 2, 4])
        mst = sb("mst", [P, 2, 32], BF16)
        mtr = sb("mtr", [P, 2, 32], BF16)
        ident = sb("ident", [P, P])
        identb = sb("identb", [P, P], BF16)
        cmat = sb("cmat", [P, P])
        gmat = sb("gmat", [P, P])
        iota = sb("iota", [P, E])
        keep = sb("keep", [P, B * 4])
        keepraw = sb("keepraw", [P, B * 4], U8)
        stats = sb("stats", [P, NT, 6])
        mv = sb("mv", [P, NT, 2])
        veps = sb("veps", [P, NT])
        sd = sb("sd", [P, NT])
        rs = sb("rs", [P, NT])
        eps6 = sb("eps6", [P, 1])
        rden = sb("rden", [P, 2, QT * HU])
        gl = [sb(f"gl{i}", [P, NT, E]) for i in range(4)]
        g8 = sb("g8", [P, NT, 8])
        gi = sb("gi", [P, NT, 8], U32)
        gif = sb("gif", [P, NT, 8])
        gs = sb("gs", [P, NT])
        gw_ = sb("gweight", [P, NT, E])
        wT = sb("wT", [E, TOK])
        mraw = att[:].rearrange("p b q c -> p (b q c)").bitcast(U8).rearrange("p (b k) -> p b k", k=SK)
        zrow = wT[0:1, :].bitcast(BF16)

        W = {}
        for p in "012":
            for n in "qkvo":
                W[n + p] = sb(f"w{n}{p}", [P, D])
            for n in "qk":
                W["b" + n + p] = sb(f"b{n}{p}", [P, 1])
            for n in "vo":
                W["b" + n + p] = sb(f"b{n}{p}", [P, D])
        lnw = sb("lnw", [P, 4])
        affine = [sb(f"affine{i}", [P, D]) for i in range(4)]
        gateW = [sb(f"gateW{i}", [P, E]) for i in range(2)]
        gateB = [sb(f"gateB{i}", [P, E]) for i in range(2)]
        b2s = [sb(f"b2s{i}", [E, D]) for i in range(2)]

        ubuf = scratch[:, 0:6 * CH].rearrange("p (j c) -> p j c", j=6)
        cbuf = scratch[:, 6 * CH:12 * CH].rearrange("p (j c) -> p j c", j=6)
        rbuf = scratch[:, 12 * CH:14 * CH].rearrange("p (j c) -> p j c", j=2)
        maskrow = scratch[0:1, 14 * CH:16 * CH].bitcast(BF16)
        maskrow_raw = scratch[0:1, 10 * CH:11 * CH].bitcast(U8)
        mkq_raw = scratch[:, 14 * CH:16 * CH].bitcast(U8).rearrange("p (b c) -> p b c", c=2 * SQ)
        prob = scratch[:].rearrange("p (r c) -> p r c", r=2)
        hid = scratch[:, 0:8 * CH].rearrange("p (r f c) -> p r f c", r=2, f=4)
        w1s = scratch[:, 8 * CH:8 * CH + 2 * (CH + 4)].rearrange("p (r c) -> p r c", r=2)
        w2s = scratch[:, 11 * CH:13 * CH].rearrange("p (r c) -> p r c", r=2)

        x_loaded, ctx_loaded, const_loaded = sem("x_loaded"), sem("ctx_loaded"), sem("const_loaded")
        masks_loaded = sem("masks_loaded")
        pool_rows = sem("pool_rows")
        pool_const = sem("pool_const")
        dve_const = sem("dve_const")
        maskrow_ready = sem("maskrow_ready")
        zerorow_ready = sem("zerorow_ready")
        mkq_ready = sem("mkq_ready")
        stored = sem("stored")
        dve_step = sem("dve_step")
        A = [Phase("ax", 4, sem, True, "key"), Phase("as", 2, sem, False, None),
             Phase("al", 4, sem, False, "full")]
        A[0].src = A[2].src = ctxT
        A[1].src = xT
        norms = NormSemaphores(sem)
        N = [Norm(i, 2 * (i - (i > 3)), NT * i + (i > 2), norms) for i in range(6)]
        gate_sems = GateSemaphores(sem)
        M = [Moe(0, 2, sem, gate_sems, ACT.Relu, 2), Moe(1, 4, sem, gate_sems, ACT.Gelu, 1)]
        identb_ready = sem("identb_ready")
        mqk_ready = sem("mqk_ready")

        bcast = lambda ap, n: ap.partition_broadcast(n)

        kept_q = nc.dram_tensor("kept_q", (B, 3 * DH, H, SQ), BF16, kind="Internal").ap()
        kept_k = {nk: nc.dram_tensor(f"kept_k{nk}", (B, 3 * DH, H, nk * P), BF16, kind="Internal").ap()
                  for nk in (2, 4)}

        block = ctx.enter_context(nc.Block())

        @block.sync
        def _(sp):
            sp.dma_start(X[:], I["x"].rearrange("(t p) d -> p t d", p=P)).then_inc(x_loaded, 16)
            sp.dma_start(maskrow_raw, I["mask0_row"]).then_inc(masks_loaded, 16)
            sp.dma_start(keepraw[:], I["mask0_col"]).then_inc(masks_loaded, 16)
            for n, t in (("ident", ident), ("cmat", cmat), ("gmat", gmat)):
                sp.dma_start(t[:], I[n]).then_inc(const_loaded, 16)
            sp.dma_start(lnw[:], I["lnw"]).then_inc(const_loaded, 16)
            sp.dma_start(ctxT[:], I["ctxT"]).then_inc(ctx_loaded, 16)
            for i, a in enumerate(A):
                for n in "qkvo":
                    sp.dma_start(W[f"{n}{i}"][:], I[f"w{n}{i}"]).then_inc(a.w_loaded, 16)
                for n in "qk":
                    sp.dma_start(W[f"b{n}{i}"][:], I[f"b{n}{i}"]).then_inc(a.w_loaded, 16)
                for n in "vo":
                    sp.dma_start(W[f"b{n}{i}"][:], bcast(I[f"b{n}{i}"], P)).then_inc(a.w_loaded, 16)
            for i in range(4):
                sp.dma_start(affine[i][:], bcast(I[f"affine{i}"], P)).then_inc(const_loaded, 16)
            for i, m in enumerate(M):
                sp.dma_start(gateW[i][:], I[f"gateW{i}"]).then_inc(m.small_loaded, 16)
                sp.dma_start(gateB[i][:], bcast(I[f"gateB{i}"], P)).then_inc(m.small_loaded, 16)
                sp.dma_start(b2s[i][:], I[f"b2{i}"]).then_inc(m.small_loaded, 16)
            sp.dma_start(mraw, I["mask1_qk"]).then_inc(masks_loaded, 16)

            def place_parts(a):
                def place(j):
                    sp.wait_ge(a.kept[j % 2], kept_total(a, j))
                    k = a.jobs[j][0] == "k"
                    op = (Kop if a.nk == 4 else Kself) if k else Qop
                    back = (kept_k[a.nk] if k else kept_q)
                    for b in batches(a, j)[0]:
                        for first, n in (K_RUNS if k else [(t, 1) for t in range(len(QPART))]):
                            part = (KPART if k else QPART)[first]
                            sp.dma_start(op[first * DH:(first + n) * DH, b * H:(b + 1) * H, :],
                                         back[b, part * DH:(part + n) * DH, :, :]).then_inc(a.placed, 16)

                for j, (kind, c) in enumerate(a.jobs):
                    sp.wait_ge(a.parts_ready, j + 1)
                    bs, w = batches(a, j)
                    back = kept_k[a.nk] if kind == "k" else kept_q
                    for i, b in enumerate(bs):
                        sp.dma_start(back[b].rearrange("(s d) h t -> (d h) s t", s=3),
                                     parts[:, j % 2, :, i * w:(i + 1) * w]).then_inc(a.kept[j % 2], 16)
                    if j:
                        place(j - 1)
                place(len(a.jobs) - 1)

            def place_max(a, u, par, half):
                sp.wait_ge(a.max_row, u + 1)
                for g in range(4):
                    dst = Qop[ROW_MAX:ROW_MAX + 1, bass.ds(u * HU, HU), :].rearrange(
                        "o h (q g j) -> o (h q) g j", q=QT, g=4)[:, :, g, :]
                    sp.dma_start(dst, mtr[32 * g:32 * g + HU * QT, par, :]).then_inc(a.max_placed[par], 16)

            def attention(a):
                if a.mask == "key":
                    sp.wait_ge(pool_rows, B + 1)
                    for half in range(2):
                        sp.dma_start(Kop[ROW_MAX:ROW_MAX + 1, half * 32:(half + 1) * 32, :].rearrange("o a k -> o (a k)").bitcast(F32),
                                     I["minus_ones"]).then_inc(a.maskrow_placed, 16)
                    sp.wait_ge(maskrow_ready, 1)
                    for h in range(H):
                        sp.dma_start(
                            Kop[ROW_MASK:ROW_MASK + 1, :, :].rearrange("o (b h) k -> o b h k", h=H)[:, :, h, :],
                            maskrow.rearrange("o (b k) -> o b k", b=B)).then_inc(a.maskrow_placed, 16)
                place_parts(a)
                place_max(a, 0, 0, 0)
                place_max(a, 1, 1, 0)
                with sp.Fori(1, UNITS // 2) as k:
                    place_max(a, 2 * k, 0, k)
                    place_max(a, 2 * k + 1, 1, k)

            def experts(i, m):
                def load(e, slot, name):
                    w = m.ft * P
                    sp.dma_start(w1s[:, slot, 0:w + m.ft], I[f"w1{i}"][bass.ds(e, 1), :, :].rearrange("e p f -> p (e f)")).then_inc(m.w_loaded[slot], 16)
                    sp.dma_start(w2s[:, slot, 0:w], I[f"w2{i}"][bass.ds(e, 1), :, :].rearrange("e p f -> p (e f)")).then_inc(m.w_loaded[slot], 16)
                load(0, 0, "")
                load(1, 1, "")
                with sp.Fori(1, E // 2) as k:
                    sp.wait_ge(m.down_ps, (2 * k - 1) * NT)
                    load(2 * k, 0, "")
                    sp.wait_ge(m.down_ps, 2 * k * NT)
                    load(2 * k + 1, 1, "")

            attention(A[0])
            sp.wait_ge(A[0].pv_done, UNITS)
            sp.dma_start(mkq_raw, I["mask1_kq"]).then_inc(masks_loaded, 16)
            sp.wait_ge(zerorow_ready, 1)
            for h in range(H):
                sp.dma_start(
                    Kop[ROW_MASK:ROW_MASK + 1, :, :].rearrange("o (b h) k -> o b h k", h=H)[:, :, h, :],
                    zrow.rearrange("o (b k) -> o b k", b=B)).then_inc(A[1].maskrow_placed, 16)
            attention(A[1])
            sp.wait_ge(A[1].pv_done, UNITS)
            experts(0, M[0])
            sp.wait_ge(M[0].down_ps, E * NT)
            attention(A[2])
            sp.wait_ge(A[2].pv_done, UNITS)
            experts(1, M[1])
            sp.wait_ge(M[1].down_done, E * NT)
            sp.dma_start(out.rearrange("(t p) d -> p t d", p=P), XB[:]).then_inc(stored, 16)
            sp.wait_ge(stored, 16)

        @block.gpsimd
        def _(pool):
            for b in range(B):
                nc.gpsimd.memset(Kop[:, b * H:(b + 1) * H, :].bitcast(F32), 0.0).then_inc(pool_rows, 1)
            nc.gpsimd.memset(Qop[:].bitcast(F32), ONES_PAIR).then_inc(pool_rows, 1)
            nc.gpsimd.memset(Vcur[:], 0.0)
            nc.gpsimd.memset(mst[:], 0.0)
            nc.gpsimd.memset(eps6[:], 1e-6)
            nc.gpsimd.memset(zrow, 0.0).then_inc(zerorow_ready, 1)
            for e in range(E):
                nc.gpsimd.memset(iota[:, e:e + 1], float(e))
            nc.gpsimd.memset(Vall[:], 1.0).then_inc(pool_const, 1)
            pool.wait_ge(masks_loaded, 16 * 3)
            nc.gpsimd.tensor_scalar(mqk[:], mraw, MASKED, None,
                                    ALU.mult).then_inc(mqk_ready, 1)

            def stage(a, u, par, first=False):
                if not first:
                    pool.wait_ge(a.pv_done, u - 1)
                src = Vall[:, bass.ds(u * HU, HU), 0:a.nk, :].rearrange("p h k d -> p k h d")
                last = nc.gpsimd.tensor_copy(Vcur[:, par, 0:a.nk, :, 0:DH + 1], src)
                last.then_inc(a.vcur_ready, 1)

            def stage_mask(a, u, par, first=False):
                if a.mask == "full":
                    if not first:
                        pool.wait_ge(a.max_row, u - 1)
                    nc.gpsimd.tensor_copy(mcur[:, par, :, :], mqk[:, bass.ds(u // UPB * QT, QT), :]).then_inc(a.mcur_ready, 1)

            for a in A:
                if a.mask == "key":
                    pool.wait_ge(a.v_ready, a.vt)
                    pool.wait_ge(dve_const, 1)
                    for t in range(a.vt):
                        b, k = divmod(t, a.nk)
                        v = Vall[:, b * H:(b + 1) * H, k, :]
                        nc.gpsimd.tensor_scalar(v, v, keep[:, t:t + 1], None, ALU.mult).then_inc(a.v_masked, 1)
                    pool.wait_ge(a.v_masked, a.vt)
                else:
                    pool.wait_ge(a.v_ready, a.vt)
                stage_mask(a, 0, 0, True)
                stage_mask(a, 1, 1, True)
                stage(a, 0, 0, True)
                stage(a, 1, 1, True)
                stage_mask(a, 2, 0)
                stage_mask(a, 3, 1)
                stage_mask(a, 4, 0)
                stage_mask(a, 5, 1)
                with pool.Fori(1, UNITS // 2 - 2) as k:
                    stage(a, 2 * k, 0)
                    stage_mask(a, 2 * k + 4, 0)
                    stage(a, 2 * k + 1, 1)
                    stage_mask(a, 2 * k + 5, 1)
                stage(a, UNITS - 4, 0)
                stage(a, UNITS - 3, 1)
                stage(a, UNITS - 2, 0)
                stage(a, UNITS - 1, 1)
                if a.mask == "key":
                    pool.wait_ge(a.vcur_ready, UNITS)
                    nc.gpsimd.memset(Vall[:], 1.0).then_inc(pool_const, 1)

        @block.scalar
        def _(act):
            def norm_sd(n):
                act.wait_ge(n.var_ready, n.i + 1)
                nc.scalar.activation(sd[:], veps[:], ACT.Sqrt).then_inc(n.sd_ready, 1)

            def norm_transposed(n):
                for half in range(2):
                    act.wait_ge(n.t_ps, n.half0 + half + 1)
                    nc.scalar.copy(xT[:, half * CH:(half + 1) * CH], PS[:, 6 + half, :]).then_inc(n.t_ready, 1)

            def prepare(a):
                nj = len(a.jobs)
                if a.qk_norm:
                    act.wait_ge(pool_const, 1)
                    for j in range(nj):
                        act.wait_ge(a.cent_ready, j + 1)
                        nc.scalar.copy(cbuf[:, j, :], PS[:, j, :])
                        nc.scalar.activation(ubuf[:, j, :], PS[:, j, :], ACT.Square).then_inc(a.sq_ready, 1)
                    for j in range(nj):
                        act.wait_ge(a.var_ready, j + 1)
                        nc.scalar.activation(ubuf[:, j, :], PS[:, j, :], ACT.Sqrt, bias=eps6[:]).then_inc(a.sd_ready, 1)
                for j in range(nj):
                    r = j % 2
                    act.wait_ge(a.full_ready, j + 1)
                    if j >= 2:
                        act.wait_ge(a.kept[r], kept_total(a, j - 2))
                    nc.scalar.copy(parts[:, r, 0, :], ubuf[:, j, :]).then_inc(a.hi_ready, 1)
                    act.wait_ge(a.rest_ready, j + 1)
                    nc.scalar.copy(parts[:, r, 1, :], rbuf[:, r, :]).then_inc(a.mid_ready, 1)

            def exps(a, u, par, first=False):
                if not first:
                    act.wait_ge(a.pv_done, u - 1)
                for s in range(2 * a.nk):
                    act.wait_ge(a.st_ps, u * 2 * a.nk + s + 1)
                    nc.scalar.activation(prob[:, par, s * CH:(s + 1) * CH], PS[:, 4 + s % 2, :],
                                         ACT.Exp).then_inc(a.exp_done, 1)

            def evacuate(a, u, par, first=False):
                act.wait_ge(a.pv_done, u + 1)
                if not first:
                    act.wait_ge(a.ot_ps, u - 1)
                nc.scalar.copy(osb[:, par, :], PS[:, 6, 0:SQ]).then_inc(a.o_ready, 1)

            def attention(i, a):
                exps(a, 0, 0, True)
                exps(a, 1, 1, True)
                evacuate(a, 0, 0, True)
                exps(a, 2, 0)
                evacuate(a, 1, 1, True)
                with act.Fori(1, UNITS // 2 - 1) as k:
                    exps(a, 2 * k + 1, 1)
                    evacuate(a, 2 * k, 0)
                    exps(a, 2 * k + 2, 0)
                    evacuate(a, 2 * k + 1, 1)
                exps(a, UNITS - 1, 1)
                evacuate(a, UNITS - 2, 0)
                evacuate(a, UNITS - 1, 1)
                for half in range(2):
                    act.wait_ge(a.att_ps, half + 1)
                    nc.scalar.mul(xT[:, half * CH:(half + 1) * CH], PS[:, half, :],
                                  ISQ if i == 2 else 1.0).then_inc(a.att_ready, 1)

            def gates(m):
                act.wait_ge(m.gates.shifted, m.i + 1)
                nc.scalar.activation(gl[1][:], gl[0][:], ACT.Exp).then_inc(m.gates.gate_exp, 1)
                act.wait_ge(m.gates.wt_ps, m.i + 1)
                nc.scalar.copy(wT[:].rearrange("e (a c) -> e a c", a=2), PS[0:E, 1:3, :]).then_inc(m.gates.wt_ready, 1)

            def experts(i, m):
                def hidden(e, j, n0):
                    c = j % 2
                    if n0 is not None:
                        act.wait_ge(m.down_ps, n0)
                    for f in range(m.ft):
                        act.wait_ge(m.up_ps, (e * 2 + c) * m.ft + f + 1)
                        bank = (j * m.ft + f) % 4
                        nc.scalar.activation(hid[:, c, f, :], PS[:, bank, :], m.act,
                                             bias=w1s[:, j // 2, m.ft * P + f:m.ft * P + f + 1]).then_inc(m.hid_ready, 1)
                hidden(0, 0, None)
                hidden(0, 1, None)
                hidden(1, 2, 4)
                hidden(1, 3, 8)
                with act.Fori(1, E // 2) as k:
                    for j in range(4):
                        hidden(2 * k + j // 2, j, k * 16 + 4 * (j - 1))

            act.wait_ge(const_loaded, 16 * 8)
            nc.scalar.copy(identb[:], ident[:]).then_inc(identb_ready, 1)
            norm_sd(N[0])
            norm_transposed(N[0])
            prepare(A[0])
            attention(0, A[0])
            norm_sd(N[1])
            norm_transposed(N[1])
            prepare(A[1])
            attention(1, A[1])
            norm_sd(N[2])
            norm_transposed(N[2])
            gates(M[0])
            experts(0, M[0])
            norm_sd(N[3])
            norm_sd(N[4])
            norm_transposed(N[4])
            prepare(A[2])
            attention(2, A[2])
            norm_sd(N[5])
            norm_transposed(N[5])
            gates(M[1])
            experts(1, M[1])

        @block.vector
        def _(dve):
            steps = [0]

            def link(ins):
                steps[0] += 1
                ins.then_inc(dve_step, 1)
                dve.wait_ge(dve_step, steps[0])

            def count(ins):
                steps[0] += 1
                ins.then_inc(dve_step, 1)

            def sync():
                dve.wait_ge(dve_step, steps[0])

            V = nc.vector

            def over_tiles(t):
                return t[:].unsqueeze(1).to_broadcast([P, NT, D])

            def norm(n, src, dst, transposed=True):
                for t in range(NT):
                    count(V.bn_stats(stats[:, t, :], src[:, t, :]))
                sync()
                for t in range(NT):
                    count(V.bn_aggr(mv[:, t, :], stats[:, t, :]))
                sync()
                V.tensor_scalar(veps[:], mv[:, :, 1], 1e-5, None, ALU.add).then_inc(n.var_ready, 1)
                dve.wait_ge(n.sd_ready, n.i + 1)
                link(V.reciprocal(rs[:], sd[:]))
                for t in range(NT):
                    V.tensor_scalar(dst[:, t, :], src[:, t, :], mv[:, t, 0:1], rs[:, t:t + 1],
                                    ALU.subtract, ALU.mult).then_inc(n.done, 1)
                dve.wait_ge(n.done, n.tile0 + NT)

            def prepare(i, a):
                nj = len(a.jobs)
                dve.wait_ge(a.w_loaded, 16 * 8)
                for j, (kind, c) in enumerate(a.jobs):
                    dve.wait_ge(a.proj_ready, j + 1)
                    scale = ISQ if (kind == "q" and i == 1) else 1.0
                    ins = V.tensor_scalar(ubuf[:, j, :], PS[:, j, :], W[f"b{kind}{i}"][:], scale,
                                          ALU.add, ALU.mult)
                    ins.then_inc(a.u_ready if a.qk_norm else a.full_ready, 1)
                if a.qk_norm:
                    for j, (kind, c) in enumerate(a.jobs):
                        dve.wait_ge(a.sd_ready, j + 1)
                        link(V.reciprocal(ubuf[:, j, :], ubuf[:, j, :]))
                        link(V.tensor_tensor(cbuf[:, j, :], cbuf[:, j, :], ubuf[:, j, :], ALU.mult))
                        o = 0 if kind == "q" else 2
                        ins = V.tensor_scalar(ubuf[:, j, :], cbuf[:, j, :], lnw[:, o:o + 1],
                                              lnw[:, o + 1:o + 2], ALU.mult, ALU.add)
                        ins.then_inc(a.full_ready, 1)
                        split(a, j)
                else:
                    for j in range(nj):
                        split(a, j)

            def split(a, j):
                r = j % 2
                dve.wait_ge(a.hi_ready, j + 1)
                V.tensor_tensor(rbuf[:, r, :], ubuf[:, j, :], parts[:, r, 0, :],
                                ALU.subtract).then_inc(a.rest_ready, 1)
                dve.wait_ge(a.mid_ready, j + 1)
                V.tensor_tensor(parts[:, r, 2, :], rbuf[:, r, :], parts[:, r, 1, :],
                                ALU.subtract).then_inc(a.parts_ready, 1)

            def values(i, a):
                if i == 0:
                    dve.wait_ge(pool_const, 1)
                if i == 1:
                    dve.wait_ge(pool_const, 2)
                for t in range(a.vt):
                    b, k = divmod(t, a.nk)
                    if t % 4 == 0:
                        dve.wait_ge(a.v_ps, t // 4 + 1)
                    V.tensor_tensor(Vall[:, b * H:(b + 1) * H, k, 0:DH],
                                    PS[:, 6 + t // 4 % 2, t % 4 * D:(t % 4 + 1) * D].rearrange("p (h d) -> p h d", d=DH),
                                    W[f"bv{i}"][:].rearrange("p (h d) -> p h d", d=DH), ALU.add).then_inc(a.v_ready, 1)

            def maxima(a, u, par, first=False, finish=False):
                if not first:
                    dve.wait_ge(a.max_row, u - 1)
                if a.mask == "full":
                    dve.wait_ge(a.mcur_ready, u + 1)
                    dve.wait_ge(mqk_ready, 1)
                    for s in range(2 * a.nk):
                        if finish and s == a.nk:
                            normalise(a, u - LEAD - 2, 1 - par)
                        if s % 2 == 0:
                            dve.wait_ge(a.max_ps, u * 2 * a.nk + s + 2)
                            V.memset(gate[:, par, s // 2:s // 2 + 1], 0.0)
                        V.tensor_tensor_reduce(out=junk[:, s % 4, :], in0=PS[:, s % 4, :], in1=mcur[:, par, s % 2, :],
                                               scale=1.0, scalar=LOWEST, op0=ALU.add, op1=ALU.max,
                                               accum_out=mstf[:, par, s:s + 1]).then_inc(
                                                   a.max_done if s % 2 else a.max_half, 1)
                    dve.wait_ge(a.max_done, (u + 1) * a.nk)
                    V.tensor_copy(mst[:, par, 0:2 * a.nk], mstf[:, par, 0:2 * a.nk]).then_inc(a.max_col, 1)
                    dve.wait_ge(a.max_col, u + 1)
                else:
                    for p in range(a.nk):
                        if finish and p == a.nk // 2:
                            normalise(a, u - LEAD - 2, 1 - par)
                        dve.wait_ge(a.max_ps, u * 2 * a.nk + 2 * p + 2)
                        banks = PS[:, p % 2 * 2:p % 2 * 2 + 2, :]
                        if a.nk == 4:
                            V.tensor_reduce(mst[:, par, 2 * p:2 * p + 2], banks, AX.X, ALU.max).then_inc(a.max_done, 1)
                        else:
                            V.tensor_reduce(mst[:, par, 4 * p:4 * p + 4].rearrange("p (i q) -> p q i", q=2),
                                            banks.rearrange("p q (i k) -> p q i k", i=2), AX.X,
                                            ALU.max).then_inc(a.max_done, 1)
                    dve.wait_ge(a.max_done, (u + 1) * a.nk)
                if not first:
                    dve.wait_ge(a.max_placed[par], (u - par) * 32)
                V.transpose(mtr[:, par, :], mst[:, par, :]).then_inc(a.max_row, 1)

            def normalise(a, u, par, first=False):
                dve.wait_ge(a.ot_ps, u + 1)
                o = PS[:, 7, :].rearrange("p (r q h c) -> p r q h c", r=2, q=QT, h=HU)[:, 0]
                rd = rden[:, par, :].rearrange("p (q h) -> p q h", q=QT)
                V.reciprocal(rd, o[:, :, :, DH]).then_inc(a.rd_ready, 1)
                dve.wait_ge(a.rd_ready, u + 1)
                dst = att[:, bass.ds(u // UPB, 1), :, bass.ds(u % UPB * HU * DH, HU * DH)].rearrange(
                    "p b q (h d) -> p (b q) h d", h=HU)
                V.tensor_tensor(dst, o[:, :, :, 0:DH],
                                rd.unsqueeze(3).to_broadcast([P, QT, HU, DH]), ALU.mult).then_inc(a.norm_done, 1)

            def attention(i, a):
                maxima(a, 0, 0, True)
                maxima(a, 1, 1, True)
                maxima(a, 2, 0)
                maxima(a, 3, 1)
                maxima(a, 4, 0)
                if i == 0:
                    dve.wait_ge(mqk_ready, 1)
                maxima(a, 5, 1, finish=True)
                with dve.Fori(1, UNITS // 2 - 2) as k:
                    maxima(a, 2 * k + 4, 0, finish=True)
                    maxima(a, 2 * k + 5, 1, finish=True)
                for u in range(UNITS - LEAD - 2, UNITS):
                    normalise(a, u, u % 2)

            def project_out(i, a, res, dst):
                for t in range(NT):
                    dve.wait_ge(a.out_ps, t // 4 + 1)
                    V.tensor_tensor(dst[:, t, :], PS[:, 2 + t // 4, t % 4 * D:(t % 4 + 1) * D], res[:, t, :],
                                    ALU.add).then_inc(a.out_done, 1)
                dve.wait_ge(a.out_done, NT)

            def gates(i, m, res):
                g0, g1, g2, g3 = (g[:] for g in gl)
                dve.wait_ge(m.small_loaded, 16 * 3)
                dve.wait_ge(m.gates.logit_ps, m.i + 1)
                gb = gateB[i][:].unsqueeze(1).to_broadcast([P, NT, E])
                link(V.tensor_tensor(g2, PS[:, 0, 0:NT * E].rearrange("p (t e) -> p t e", e=E), gb, ALU.add))
                link(V.tensor_reduce(gs[:], g2, AX.X, ALU.max))
                per = gs[:].unsqueeze(2).to_broadcast([P, NT, E])
                V.tensor_tensor(g0, g2, per, ALU.subtract).then_inc(m.gates.shifted, 1)
                dve.wait_ge(m.gates.gate_exp, m.i + 1)
                link(V.tensor_reduce(gs[:], g1, AX.X, ALU.add))
                link(V.reciprocal(rs[:], gs[:]))
                link(V.tensor_tensor(g2, g1, rs[:].unsqueeze(2).to_broadcast([P, NT, E]), ALU.mult))
                for t in range(NT):
                    count(V.max(g8[:, t, :], gl[2][:, t, :]))
                sync()
                for t in range(NT):
                    count(V.max_index(gi[:, t, :], g8[:, t, :], gl[2][:, t, :]))
                sync()
                link(V.tensor_copy(gif[:], gi[:]))
                io = iota[:].unsqueeze(1).to_broadcast([P, NT, E])
                pick = lambda k: gif[:, :, k:k + 1].to_broadcast([P, NT, E])
                if m.topk == 1:
                    V.tensor_tensor(gw_[:], io, pick(0), ALU.is_equal).then_inc(m.gates.weight_ready, 1)
                else:
                    link(V.tensor_tensor(g3, io, pick(0), ALU.is_equal))
                    link(V.tensor_tensor(g0, io, pick(1), ALU.is_equal))
                    link(V.tensor_tensor(g3, g3, g0, ALU.add))
                    V.tensor_tensor(gw_[:], g3, g2, ALU.mult).then_inc(m.gates.weight_ready, 1)
                dve.wait_ge(m.gates.weight_ready, m.i + 1)
                dve.wait_ge(m.gates.b2_ps, m.i + 1)
                V.tensor_tensor(XB[:], PS[:, 3:5, :].rearrange("p a (t d) -> p (a t) d", d=D), res[:],
                                ALU.add).then_inc(m.gates.acc_ready, 1)
                dve.wait_ge(m.gates.acc_ready, m.i + 1)

            def experts(i, m):
                def add(e, first=False):
                    for t in range(NT):
                        n = e * NT + t
                        dve.wait_ge(m.down_ps, n + 1)
                        if not first:
                            dve.wait_ge(m.down_done, n + 1 - NT)
                        V.scalar_tensor_tensor(XB[:, t, :], PS[:, 4 + t % 4, 0:D],
                                               gw_[:, t, bass.ds(e, 1)], XB[:, t, :],
                                               ALU.mult, ALU.add).then_inc(m.down_done, 1)
                add(0, True)
                with dve.Fori(1, E) as e:
                    add(e)
                dve.wait_ge(m.down_done, E * NT)

            dve.wait_ge(masks_loaded, 16 * 3)
            V.tensor_copy(keep[:], keepraw[:]).then_inc(dve_const, 1)
            link(V.tensor_copy(maskrow, maskrow_raw))
            V.tensor_scalar(maskrow, maskrow, 1.0, -MASKED, ALU.subtract, ALU.mult).then_inc(maskrow_ready, 1)
            dve.wait_ge(maskrow_ready, 1)

            dve.wait_ge(x_loaded, 16)
            norm(N[0], X, XN)
            dve.wait_ge(const_loaded, 16 * 8)
            link(V.tensor_scalar(lnw[:, 0:2], lnw[:, 0:2], ISQ, None, ALU.mult))
            prepare(0, A[0])
            values(0, A[0])
            link(V.tensor_tensor(XB[:], X[:], over_tiles(W["bo0"]), ALU.add))
            attention(0, A[0])
            project_out(0, A[0], XB, X)
            norm(N[1], X, XN)
            dve.wait_ge(A[1].w_loaded, 16 * 8)
            link(V.tensor_tensor(XB[:], XN[:], over_tiles(W["bo1"]), ALU.add))
            prepare(1, A[1])
            values(1, A[1])
            dve.wait_ge(masks_loaded, 16 * 4)
            V.tensor_scalar(mkq[:], mkq_raw, MASKED, None, ALU.mult).then_inc(mkq_ready, 1)
            attention(1, A[1])
            project_out(1, A[1], XB, XB)
            norm(N[2], XB, XN)
            link(V.tensor_tensor(XN[:], XN[:], over_tiles(affine[0]), ALU.mult))
            V.tensor_tensor(XN[:], XN[:], over_tiles(affine[1]), ALU.add).then_inc(N[2].done, 1)
            dve.wait_ge(N[2].done, N[2].tile0 + NT + 1)
            gates(0, M[0], XN)
            experts(0, M[0])
            norm(N[3], XB, XN)
            link(V.tensor_tensor(XN[:], XN[:], over_tiles(affine[2]), ALU.mult))
            link(V.tensor_tensor(XN[:], XN[:], over_tiles(affine[3]), ALU.add))
            link(V.tensor_tensor(X[:], X[:], XN[:], ALU.add))
            norm(N[4], X, XN)
            dve.wait_ge(A[2].w_loaded, 16 * 8)
            prepare(2, A[2])
            values(2, A[2])
            link(V.tensor_tensor(XB[:], X[:], over_tiles(W["bo2"]), ALU.add))
            attention(2, A[2])
            project_out(2, A[2], XB, X)
            norm(N[5], X, XN)
            gates(1, M[1], X)
            experts(1, M[1])

        @block.tensor
        def _(pe):
            mm = nc.tensor.matmul

            def norm_transpose(n, extra=0):
                pe.wait_ge(const_loaded, 16 * 8)
                for half in range(2):
                    pe.wait_ge(n.done, n.tile0 + 4 * half + 4)
                    if extra:
                        pe.wait_ge(n.done, n.tile0 + NT + extra)
                    for t in range(4 * half, 4 * half + 4):
                        last = nc.tensor.transpose(PS[:, 6 + half, t % 4 * P:(t % 4 + 1) * P], XN[:, t, :], ident[:])
                    last.then_inc(n.t_ps, 1)

            def prepare(i, a, n):
                pe.wait_ge(a.w_loaded, 16 * 8)
                pe.wait_ge(ctx_loaded, 16)
                for j, (kind, c) in enumerate(a.jobs):
                    src = xT if kind == "q" else a.src
                    if j == 0 or src is xT:
                        pe.wait_ge(n.t_ready, n.half0 + 2)
                    mm(PS[:, j, :], W[f"{kind}{i}"][:], src[:, c * CH:(c + 1) * CH], start=True, stop=True).then_inc(a.proj_ready, 1)
                if a.qk_norm:
                    for j in range(len(a.jobs)):
                        pe.wait_ge(a.u_ready, j + 1)
                        mm(PS[:, j, :], cmat[:], ubuf[:, j, :], start=True, stop=True).then_inc(a.cent_ready, 1)
                    for j in range(len(a.jobs)):
                        pe.wait_ge(a.sq_ready, j + 1)
                        mm(PS[:, j, :], gmat[:], ubuf[:, j, :], start=True, stop=True).then_inc(a.var_ready, 1)
                for t in range(a.vt):
                    if t % 4 == 0 and t >= 8:
                        pe.wait_ge(a.v_ready, t - 4)
                    last = mm(PS[:, 6 + t // 4 % 2, t % 4 * D:(t % 4 + 1) * D], a.src[:, t * P:(t + 1) * P],
                              W[f"v{i}"][:], start=True, stop=True)
                    if t % 4 == 3:
                        last.then_inc(a.v_ps, 1)

            def max_slot(a, u, s, first=False):
                n = u * 2 * a.nk + s
                if s % 2 == 0 and not (first and s < 4):
                    pe.wait_ge(a.max_done, u * a.nk + s // 2 - 1)
                bank = s % 4
                hp, q = divmod(s, 2)
                if a.nk == 4:
                    last = mm(PS[:, bank, :], unit_head(Qop, u, hp, ROW_MAX, q * P, P),
                              unit_head(Kop, u, hp, ROW_MAX, 0, SK), start=True, stop=True)
                else:
                    for i in range(2):
                        last = mm(PS[:, bank, i * SQ:(i + 1) * SQ], unit_head(Qop, u, 2 * hp + i, ROW_MAX, q * P, P),
                                  unit_head(Kself, u, 2 * hp + i, ROW_MAX, 0, SQ), start=True, stop=True)
                last.then_inc(a.max_ps, 1)

            def unit_head(op, u, h, rows, first, n):
                return op[0:rows, bass.ds(u * HU + h, 1), first:first + n].rearrange("p o c -> p (o c)")

            def score_slot(a, u, s, first=False):
                n = u * 2 * a.nk + s
                if not (first and s < 2):
                    pe.wait_ge(a.exp_done, n - 1)
                bank = 4 + s % 2
                h, kt0 = divmod(2 * s, a.nk)
                K = Kop if a.nk == 4 else Kself
                if a.mask == "full":
                    mm(PS[:, bank, :], identb[:], mkq[:, bass.ds(u // UPB * 2 + s % 2, 1), :].rearrange("p o k -> p (o k)"),
                       start=True, stop=False, skip_group_check=True)
                for kk in range(2):
                    last = mm(PS[:, bank, kk * SQ:(kk + 1) * SQ],
                              unit_head(K, u, h, KROWS, (kt0 + kk) * P, P), unit_head(Qop, u, h, KROWS, 0, SQ),
                              start=a.mask != "full", stop=True, skip_group_check=True)
                last.then_inc(a.st_ps, 1)

            def value_tile(a, u, par, kt):
                for h in range(HU):
                    last = mm(PS[32 * h:32 * h + 32, 6, 0:SQ], Vcur[:, par, kt, h, :],
                              prob[:, par, (h * a.nk + kt) * SQ:(h * a.nk + kt + 1) * SQ],
                              start=kt == 0, stop=kt == a.nk - 1)
                if kt == a.nk - 1:
                    last.then_inc(a.pv_done, 1)

            def to_tokens(a, u, par, first=False):
                pe.wait_ge(a.o_ready, u + 1)
                if not first:
                    pe.wait_ge(a.norm_done, u)
                for q in range(QT):
                    last = nc.tensor.transpose(PS[:, 7, q * P:(q + 1) * P], osb[:, par, q * P:(q + 1) * P], ident[:])
                last.then_inc(a.ot_ps, 1)

            def step(a, u, par, half, maxes=True, scores=True, values=True, tokens=True, first=False, ftok=False):
                if scores:
                    pe.wait_ge(a.max_placed[par], half * 64 + 64)
                for i in range(a.nk):
                    if tokens and i == a.nk // 2:
                        to_tokens(a, u - 2, par, ftok)
                    for s in (2 * i, 2 * i + 1):
                        if maxes:
                            max_slot(a, u + LEAD, s)
                        if scores:
                            score_slot(a, u, s, first)
                    if values:
                        if i == 0:
                            pe.wait_ge(a.exp_done, u * 2 * a.nk)
                            pe.wait_ge(a.vcur_ready, u)
                            if not first_values(u):
                                pe.wait_ge(a.o_ready, u - 1)
                        value_tile(a, u - 1, 1 - par, i)

            def first_values(u):
                return isinstance(u, int) and u == 1

            def attention(i, a):
                pe.wait_ge(a.placed, placed_total(a))
                if i < 2:
                    pe.wait_ge(a.maskrow_placed, 16 * (H + 2 * (i == 0)))
                pe.wait_ge(a.v_ready, a.vt)
                if i == 1:
                    pe.wait_ge(mkq_ready, 1)
                for u in range(LEAD):
                    for s in range(2 * a.nk):
                        max_slot(a, u, s, first=u == 0)
                step(a, 0, 0, 0, values=False, tokens=False, first=True)
                step(a, 1, 1, 0, tokens=False)
                step(a, 2, 0, 1, ftok=True)
                with pe.Fori(1, UNITS // 2 - 2) as k:
                    step(a, 2 * k + 1, 1, k)
                    step(a, 2 * k + 2, 0, k + 1)
                step(a, UNITS - 3, 1, UNITS // 2 - 2, maxes=False)
                step(a, UNITS - 2, 0, UNITS // 2 - 1, maxes=False)
                step(a, UNITS - 1, 1, UNITS // 2 - 1, maxes=False)
                step(a, UNITS, 0, 0, maxes=False, scores=False)
                to_tokens(a, UNITS - 1, 1)
                pe.wait_ge(a.norm_done, UNITS)
                for half in range(2):
                    for t in range(4 * half, 4 * half + 4):
                        last = nc.tensor.transpose(PS[:, half, t % 4 * P:(t % 4 + 1) * P], att[:, t // QT, t % QT, :], ident[:])
                    last.then_inc(a.att_ps, 1)
                for t in range(NT):
                    if t % 4 == 0:
                        pe.wait_ge(a.att_ready, t // 4 + 1)
                    last = mm(PS[:, 2 + t // 4, t % 4 * D:(t % 4 + 1) * D], xT[:, t * P:(t + 1) * P], W[f"o{i}"][:],
                       start=True, stop=True)
                    if t % 4 == 3:
                        last.then_inc(a.out_ps, 1)

            def gates(i, m, n):
                pe.wait_ge(m.small_loaded, 16 * 3)
                pe.wait_ge(n.t_ready, n.half0 + 2)
                for t in range(NT):
                    last = mm(PS[:, 0, t * E:(t + 1) * E], xT[:, t * P:(t + 1) * P], gateW[i][:], start=True, stop=True)
                last.then_inc(m.gates.logit_ps, 1)
                pe.wait_ge(m.gates.weight_ready, m.i + 1)
                for t in range(NT):
                    last = nc.tensor.transpose(PS[0:E, 1 + t // 4, t % 4 * P:(t % 4 + 1) * P], gw_[:, t, :], ident[:])
                last.then_inc(m.gates.wt_ps, 1)
                pe.wait_ge(m.gates.wt_ready, m.i + 1)
                for t in range(NT):
                    last = mm(PS[:, 3 + t // 4, t % 4 * D:(t % 4 + 1) * D], wT[:, t * P:(t + 1) * P], b2s[i][:], start=True, stop=True)
                last.then_inc(m.gates.b2_ps, 1)
                pe.wait_ge(m.gates.acc_ready, m.i + 1)

            def experts(i, m):
                def up(e, j, first=False):
                    c = j % 2
                    if c == 0:
                        pe.wait_ge(m.w_loaded[j // 2], (e - j // 2) * 16 + 32)
                    for f in range(m.ft):
                        n = (e * 2 + c) * m.ft + f
                        if not (first and c * m.ft + f < 4):
                            pe.wait_ge(m.hid_ready, n - 3)
                        mm(PS[:, (j * m.ft + f) % 4, :], w1s[:, j // 2, f * P:(f + 1) * P],
                           xT[:, c * CH:(c + 1) * CH], start=True, stop=True).then_inc(m.up_ps, 1)

                def down(e, j, first=False):
                    c = j % 2
                    pe.wait_ge(m.hid_ready, (e * 2 + c + 1) * m.ft)
                    for t in range(4):
                        n = e * NT + 4 * c + t
                        if not (first and c == 0):
                            pe.wait_ge(m.down_done, n - 3)
                        for f in range(m.ft):
                            last = mm(PS[:, 4 + t, 0:D], hid[:, c, f, t * P:(t + 1) * P],
                                      w2s[:, j // 2, f * D:(f + 1) * D], start=f == 0, stop=f == m.ft - 1)
                        last.then_inc(m.down_ps, 1)

                up(0, 0, True)
                up(0, 1, True)
                down(0, 0, True)
                up(1, 2)
                down(0, 1)
                up(1, 3)
                down(1, 2)
                with pe.Fori(1, E // 2) as k:
                    up(2 * k, 0)
                    down(2 * k - 1, 3)
                    up(2 * k, 1)
                    down(2 * k, 0)
                    up(2 * k + 1, 2)
                    down(2 * k, 1)
                    up(2 * k + 1, 3)
                    down(2 * k + 1, 2)
                down(E - 1, 3)

            norm_transpose(N[0])
            pe.wait_ge(identb_ready, 1)
            prepare(0, A[0], N[0])
            attention(0, A[0])
            norm_transpose(N[1])
            prepare(1, A[1], N[1])
            attention(1, A[1])
            norm_transpose(N[2], 1)
            gates(0, M[0], N[2])
            experts(0, M[0])
            norm_transpose(N[4])
            prepare(2, A[2], N[4])
            attention(2, A[2])
            norm_transpose(N[5])
            gates(1, M[1], N[5])
            experts(1, M[1])


def kernel(**inputs):
    import numpy as np
    import concourse.bacc as bacc
    from concourse.bass_utils import run_bass_kernel_spmd

    g = {k: np.asarray(v) for k, v in inputs.items()}
    rows = lambda a: np.ascontiguousarray(a)
    col = lambda a: rows(a.reshape(P, 1))
    heads = lambda a: np.repeat(a, H)
    by_dim = lambda a: rows(a.reshape(-1, H, DH).transpose(0, 2, 1).reshape(-1, D))
    centre = np.kron(np.eye(DH) - np.full((DH, DH), 1.0 / DH), np.eye(H)).astype(np.float32)
    mean = np.kron(np.full((DH, DH), 1.0 / DH), np.eye(H)).astype(np.float32)
    m1 = g["mask_BxSxS2_bk1"]
    m0 = g["mask_BxS2_bk0"]
    x0, xf, x1, f1 = "L0_xattn_", "L0_ffn_", "L1_xattn_", "L1_ffn_"
    Wkv, bkv = g[x0 + "Wkv"], g[x0 + "bkv"]

    def up(w, b, ft):
        return rows(np.concatenate([w, b.reshape(E, ft, P).transpose(0, 2, 1)], 2))

    def down(w, ft):
        return rows(w.reshape(E, ft, P, D).transpose(0, 2, 1, 3).reshape(E, P, ft * D))

    a = {
        "x": rows(g["x"].reshape(TOK, D)),
        "ctxT": rows(g["ctx_1024"].reshape(B * SK, D).T),
        "mask0_row": rows(m0.reshape(1, B * SK)),
        "mask0_col": rows(m0.reshape(B * SK // P, P).T),
        "mask1_qk": rows(m1.reshape(B * QT, P, SK).transpose(1, 0, 2)),
        "mask1_kq": rows(m1.reshape(B, SQ, SK // P, P).transpose(3, 0, 2, 1).reshape(P, B * 2, 2 * SQ)),
        "minus_ones": np.full((1, B * H * SK // 4), MINUS_ONES_PAIR, np.float32),
        "ident": np.eye(P, dtype=np.float32), "cmat": centre, "gmat": mean,
        "lnw": rows(np.stack([heads(g[x0 + n]) for n in ("qn_w", "qn_b", "kn_w", "kn_b")], 1)),
        "wq0": by_dim(g[x0 + "Wq"].T), "wk0": by_dim(Wkv[:D].T), "wv0": rows(Wkv[D:].T), "wo0": rows(g[x0 + "Wo"].T),
        "bq0": col(by_dim(g[x0 + "bq"])), "bk0": col(by_dim(bkv[:D])), "bv0": rows(bkv[D:]), "bo0": g[x0 + "bo"],
        "wq1": by_dim(g[xf + "Wq"]), "wk1": by_dim(g[xf + "Wk"]), "wv1": g[xf + "Wv"], "wo1": g[xf + "Wo"],
        "bq1": col(by_dim(g[xf + "bq"])), "bk1": col(by_dim(g[xf + "bk"])), "bv1": g[xf + "bv"], "bo1": g[xf + "bo"],
        "wq2": by_dim(g[x1 + "Wq"].reshape(D, D)), "wk2": by_dim(g[x1 + "Wk"].reshape(D, D)),
        "wv2": rows(g[x1 + "Wv"].reshape(D, D)), "wo2": rows(g[x1 + "Wo"].reshape(D, D)),
        "bq2": col(by_dim(g[x1 + "bq"])), "bk2": col(by_dim(g[x1 + "bk"])), "bv2": rows(g[x1 + "bv"].reshape(D)), "bo2": g[x1 + "bo"],
        "affine0": g[xf + "ln1_g"], "affine1": g[xf + "ln1_b"], "affine2": g[xf + "ln2_g"], "affine3": g[xf + "ln2_b"],
        "gateW0": g[xf + "gW"], "gateB0": g[xf + "gb"], "b20": g[xf + "b2"],
        "w10": up(g[xf + "W1"], g[xf + "b1"], 2), "w20": down(g[xf + "W2"], 2),
        "gateW1": g[f1 + "w_router"], "gateB1": g[f1 + "b_router"], "b21": g[f1 + "b2"],
        "w11": up(g[f1 + "w1"], g[f1 + "b1"], 4), "w21": down(g[f1 + "w2"], 4),
    }
    nc = bacc.Bacc("TRN2", target_bir_lowering=False, num_devices=1, dynamic_dma_scratch_size=1024)
    aps = {n: nc.dram_tensor("in_" + n, v.shape, mybir.dt.from_np(v.dtype), kind="ExternalInput").ap()
           for n, v in a.items()}
    out = nc.dram_tensor("out", (TOK, D), F32, kind="ExternalOutput").ap()
    build(nc, aps, out)
    r = run_bass_kernel_spmd(nc, [{"in_" + n: v for n, v in a.items()}], core_ids=[0])
    return r.results[0]["out"].reshape(B, SQ, D)
```

```python
import concourse.bass as bass
from concourse import mybir
from contextlib import ExitStack

F32 = mybir.dt.float32
BF16 = mybir.dt.bfloat16
U8 = mybir.dt.uint8
U32 = mybir.dt.uint32
ALU = mybir.AluOpType
ACT = mybir.ActivationFunctionType
AX = mybir.AxisListType

P = 128
B, SQ, SK, D = 4, 256, 512, 128
H, DH = 16, 8
TOK = B * SQ
NT = TOK // P
HU = 4
UPB = H // HU
UNITS = B * UPB
RING = 3
LEAD = 3
QT = SQ // P
E = 8
CH = 512
QPART = (0, 0, 0, 1, 1, 2)
KPART = (0, 1, 2, 0, 1, 0)
RUNS = ((0, 3), (3, 2), (5, 1))
ROW_MASK, ROW_MAX = 64, 96
KROWS = ROW_MAX + 1
VW = 32
MASKED = -(2.0 ** 99)
LOWEST = -3.0e38
ONES_PAIR = 1.0019378662109375
MINUS_ONES_PAIR = -1.0058441162109375
ISQ = DH ** -0.5


class Phase:

    def __init__(self, name, nk, sem, qk_norm, mask):
        self.name, self.nk, self.qk_norm, self.mask = name, nk, qk_norm, mask
        self.kw = nk * P
        kc = B * self.kw // CH
        jobs = []
        for c in range(kc):
            jobs.append(("k", c))
            if c < TOK // CH:
                jobs.append(("q", c))
        self.ahead = kc if mask == "full" else 0
        if self.ahead:
            jobs.sort()
        self.jobs = jobs
        self.vt = B * nk
        s = lambda what: sem(f"{name}_{what}")
        self.w_loaded = s("w_loaded")
        self.proj_ready = s("proj_ready")
        self.u_ready = qk_norm and s("u_ready")
        self.cent_ready = qk_norm and s("cent_ready")
        self.sq_ready = qk_norm and s("sq_ready")
        self.var_ready = qk_norm and s("var_ready")
        self.sd_ready = qk_norm and s("sd_ready")
        self.rs_ready = qk_norm and s("rs_ready")
        self.spread = qk_norm and s("spread")
        self.rs_ps = qk_norm and s("rs_ps")
        self.full_ready = s("full_ready")
        self.hi_ready = s("hi_ready")
        self.rest_ready = s("rest_ready")
        self.mid_ready = s("mid_ready")
        self.parts_ready = s("parts_ready")
        self.kept = [s(f"kept{r}") for r in range(RING)]
        self.placed = [s("placed_early"), s("placed_late")]
        self.early = max(j for j, (kind, c) in enumerate(jobs) if c * CH < 2 * (self.kw if kind == "k" else SQ)) + 1
        self.maskrow_placed = mask != "full" and s("maskrow_placed")
        self.v_ps = s("v_ps")
        self.v_ready = s("v_ready")
        self.v_masked = mask == "key" and s("v_masked")
        self.vcur_ready = s("vcur_ready")
        self.mcur_ready = mask == "full" and s("mcur_ready")
        self.max_ps = s("max_ps")
        self.max_done = s("max_done")
        self.max_half = mask == "full" and s("max_half")
        self.max_col = mask == "full" and s("max_col")
        self.max_row = s("max_row")
        self.max_placed = [s(f"max_placed{r}") for r in range(2)]
        self.st_ps = s("st_ps")
        self.exp_done = s("exp_done")
        self.pv_done = s("pv_done")
        self.o_ready = s("o_ready")
        self.ot_ps = s("ot_ps")
        self.rd_ready = s("rd_ready")
        self.norm_done = s("norm_done")
        self.att_ps = s("att_ps")
        self.att_ready = s("att_ready")
        self.out_ps = s("out_ps")
        self.out_done = s("out_done")


def batches(a, j):
    kind, c = a.jobs[j]
    w = a.kw if kind == "k" else SQ
    return range(c * CH // w, (c + 1) * CH // w), w


def kept_total(a, j):
    return sum(16 * (1 if a.jobs[i][0] == "k" else len(RUNS)) for i in range(j % RING, j + 1, RING))


def placed_total(a, late):
    jobs = range(a.early, len(a.jobs)) if late else range(a.early)
    return sum(16 * len(batches(a, j)[0]) * (len(RUNS) if a.jobs[j][0] == "k" else 1) for j in jobs)


class NormSemaphores:

    def __init__(self, sem):
        self.var_ready = sem("norm_var_ready")
        self.sd_ready = sem("norm_sd_ready")
        self.done = sem("norm_done")
        self.t_ps = sem("norm_t_ps")
        self.t_ready = sem("norm_t_ready")


class Norm:

    def __init__(self, i, halves_before, tiles_before, shared):
        self.i, self.half0, self.tile0 = i, halves_before, tiles_before
        self.var_ready, self.sd_ready, self.done = shared.var_ready, shared.sd_ready, shared.done
        self.t_ps, self.t_ready = shared.t_ps, shared.t_ready


class GateSemaphores:

    def __init__(self, sem):
        self.logit_ps = sem("gate_logit_ps")
        self.shifted = sem("gate_shifted")
        self.gate_exp = sem("gate_exp")
        self.weight_ready = sem("gate_weight_ready")
        self.wt_ps = sem("gate_wt_ps")
        self.wt_ready = sem("gate_wt_ready")
        self.b2_ps = sem("gate_b2_ps")
        self.acc_ready = sem("gate_acc_ready")


class Moe:

    def __init__(self, i, ft, sem, gates, act, topk):
        self.i, self.ft, self.act, self.topk, self.gates = i, ft, act, topk, gates
        s = lambda what: sem(f"moe{i}_{what}")
        self.small_loaded = s("small_loaded")
        self.w_loaded = [s(f"w_loaded{r}") for r in range(2)]
        self.up_ps = s("up_ps")
        self.hid_ready = s("hid_ready")
        self.down_ps = s("down_ps")
        self.down_done = s("down_done")


def build(nc, I, out):
    ctx = ExitStack()
    with ctx:
        sb = lambda name, shape, dt=F32: ctx.enter_context(nc.sbuf_tensor(name, shape, dt))
        sem = lambda name: ctx.enter_context(nc.semaphore(name))

        PS = ctx.enter_context(nc.psum_tensor("PS", [P, 8, CH], F32))
        Kop = sb("Kop", [P, B * H, SK], BF16)
        Qop = sb("Qop", [P, B * H, SQ], BF16)
        Kself = Kop[:].rearrange("p a (c k) -> p (a c) k", k=SQ)[:, 0:B * H, :]
        scratch = sb("scratch", [P, 16 * CH])
        X = sb("X", [P, NT, D])
        XN = sb("XN", [P, NT, D])
        XB = sb("XB", [P, NT, D])
        xT = sb("xT", [P, TOK])
        ctxT = sb("ctxT", [P, B * SK])
        att = sb("att", [P, B, QT, D])
        parts = sb("parts", [P, 2, 3, CH], BF16)
        Vall = sb("Vall", [P, B * H, 4, DH + 1])
        Vcur = sb("Vcur", [P, 2, 4, HU, VW])
        mqk = sb("mqk", [P, B * QT, SK], BF16)
        mkq = sb("mkq", [P, B * 2, 2 * SQ], BF16)
        osb = sb("osb", [P, 2, SQ])
        mcur = sb("mcur", [P, 2, QT, SK], BF16)
        slots = [parts[:, 0], parts[:, 1],
                 XN[:].rearrange("p t d -> p (t d)").bitcast(BF16)[:, 0:3 * CH].rearrange("p (s c) -> p s c", s=3)]
        junk = parts[:].rearrange("p r s c -> p (r s) c")
        mstf = sb("mstf", [P, 2, 32])
        gate = sb("gate", [P, 2, 4])
        mst = sb("mst", [P, 2, 32], BF16)
        mtr = sb("mtr", [P, 2, 32], BF16)
        ident = sb("ident", [P, P])
        identb = sb("identb", [P, P], BF16)
        cmat = sb("cmat", [P, P])
        gmat = sb("gmat", [P, H])
        iota = sb("iota", [P, E])
        keep = sb("keep", [P, B * 4])
        keepraw = sb("keepraw", [P, B * 4], U8)
        stats = sb("stats", [P, NT, 6])
        mv = sb("mv", [P, NT, 2])
        veps = sb("veps", [P, NT])
        sd = sb("sd", [P, NT])
        rs = sb("rs", [P, NT])
        eps6 = sb("eps6", [P, 1])
        head_sd = sb("head_sd", [P, 6, CH // DH])
        head_rs = sb("head_rs", [P, 6, CH // DH])
        rden = sb("rden", [P, 2, QT * HU])
        gl = [sb(f"gl{i}", [P, NT, E]) for i in range(4)]
        g8 = sb("g8", [P, NT, 8])
        gi = sb("gi", [P, NT, 8], U32)
        gif = sb("gif", [P, NT, 8])
        gs = sb("gs", [P, NT])
        gw_ = sb("gweight", [P, NT, E])
        wT = sb("wT", [E, TOK])
        mraw = att[:].rearrange("p b q c -> p (b q c)").bitcast(U8).rearrange("p (b k) -> p b k", k=SK)
        zrow = wT[0:1, :].bitcast(BF16)

        W = {}
        for p in "012":
            for n in "qkvo":
                W[n + p] = sb(f"w{n}{p}", [P, D])
            for n in "qk":
                W["b" + n + p] = sb(f"b{n}{p}", [P, 1])
            for n in "vo":
                W["b" + n + p] = sb(f"b{n}{p}", [P, D])
        lnw = sb("lnw", [P, 4])
        affcol = sb("affcol", [P, 2])
        affine = [sb(f"affine{i}", [P, D]) for i in range(4)]
        gateW = [sb(f"gateW{i}", [P, E]) for i in range(2)]
        gateB = [sb(f"gateB{i}", [P, E]) for i in range(2)]
        b2s = [sb(f"b2s{i}", [E, D]) for i in range(2)]

        ubuf = scratch[:, 0:6 * CH].rearrange("p (j c) -> p j c", j=6)
        cbuf = scratch[:, 6 * CH:12 * CH].rearrange("p (j c) -> p j c", j=6)
        rbuf = scratch[:, 12 * CH:14 * CH].rearrange("p (j c) -> p j c", j=2)
        maskrow = scratch[0:1, 14 * CH:16 * CH].bitcast(BF16)
        maskrow_raw = scratch[0:1, 10 * CH:11 * CH].bitcast(U8)
        mkq_raw = scratch[:, 14 * CH:16 * CH].bitcast(U8).rearrange("p (b c) -> p b c", c=2 * SQ)
        prob = scratch[:].rearrange("p (r c) -> p r c", r=2)
        kfull = [scratch[:, c * CH:(c + 1) * CH] for c in (2, 3, 6, 7)]
        krest = scratch[:, 13 * CH:14 * CH]
        hid = scratch[:, 0:8 * CH].rearrange("p (r f c) -> p r f c", r=2, f=4)
        w1s = scratch[:, 8 * CH:8 * CH + 2 * (CH + 4)].rearrange("p (r c) -> p r c", r=2)
        w2s = scratch[:, 11 * CH:13 * CH].rearrange("p (r c) -> p r c", r=2)

        x_loaded, ctx_loaded, const_loaded = sem("x_loaded"), sem("ctx_loaded"), sem("const_loaded")
        masks_loaded, mask1_loaded = sem("masks_loaded"), sem("mask1_loaded")
        affine_loaded = sem("affine_loaded")
        pool_rows = sem("pool_rows")
        pool_const = sem("pool_const")
        dve_const = sem("dve_const")
        maskrow_ready = sem("maskrow_ready")
        zerorow_ready = sem("zerorow_ready")
        mkq_ready = sem("mkq_ready")
        stored = sem("stored")
        dve_step = sem("dve_step")
        A = [Phase("ax", 4, sem, True, "key"), Phase("as", 2, sem, False, None),
             Phase("al", 4, sem, False, "full")]
        A[0].src = A[2].src = ctxT
        A[1].src = xT
        norms = NormSemaphores(sem)
        N = [Norm(i, 2 * (i - (i > 3)), NT * i + (i > 2), norms) for i in range(6)]
        gate_sems = GateSemaphores(sem)
        M = [Moe(0, 2, sem, gate_sems, ACT.Relu, 2), Moe(1, 4, sem, gate_sems, ACT.Gelu, 1)]
        identb_ready = sem("identb_ready")
        mqk_ready = sem("mqk_ready")

        bcast = lambda ap, n: ap.partition_broadcast(n)

        kept_q = nc.dram_tensor("kept_q", (len(QPART) * DH, H, B, SQ), BF16, kind="Internal").ap()
        kept_k = {nk: nc.dram_tensor(f"kept_k{nk}", (3 * DH, H, B, nk * P), BF16, kind="Internal").ap()
                  for nk in (2, 4)}

        block = ctx.enter_context(nc.Block())

        @block.sync
        def _(sp):
            sp.dma_start(X[:], I["x"].rearrange("(t p) d -> p t d", p=P)).then_inc(x_loaded, 16)
            sp.dma_start(ident[:], I["ident"]).then_inc(const_loaded, 16)
            sp.dma_start(ctxT[:], I["ctxT"]).then_inc(ctx_loaded, 16)

            def load_weights(i, a):
                for n in "kqvo":
                    sp.dma_start(W[f"{n}{i}"][:], I[f"w{n}{i}"]).then_inc(a.w_loaded, 16)
                for n in "qk":
                    sp.dma_start(W[f"b{n}{i}"][:], I[f"b{n}{i}"]).then_inc(a.w_loaded, 16)
                for n in "vo":
                    sp.dma_start(W[f"b{n}{i}"][:], bcast(I[f"b{n}{i}"], P)).then_inc(a.w_loaded, 16)

            load_weights(0, A[0])
            for n, t in (("cmat", cmat), ("gmat", gmat), ("lnw", lnw)):
                sp.dma_start(t[:], I[n]).then_inc(const_loaded, 16)
            sp.dma_start(maskrow_raw, I["mask0_row"]).then_inc(masks_loaded, 16)
            sp.dma_start(keepraw[:], I["mask0_col"]).then_inc(masks_loaded, 16)
            sp.dma_start(mraw, I["mask1_qk"]).then_inc(mask1_loaded, 16)

            def store(a, j):
                kind, c = a.jobs[j]
                sp.wait_ge(a.parts_ready, j + 1)
                back = (kept_k[a.nk] if kind == "k" else kept_q).rearrange("(s d) h b t -> (d h) s (b t)", d=DH)
                back = back[:, :, c * CH:(c + 1) * CH]
                if kind == "k":
                    sp.dma_start(back, slots[j % RING]).then_inc(a.kept[j % RING], 16)
                else:
                    for part, (first, n) in enumerate(RUNS):
                        sp.dma_start(back[:, first:first + n, :],
                                     slots[j % RING][:, part:part + 1, :].to_broadcast([P, n, CH])).then_inc(a.kept[j % RING], 16)

            def place(a, j):
                sp.wait_ge(a.kept[j % RING], kept_total(a, j))
                bs = batches(a, j)[0]
                k = a.jobs[j][0] == "k"
                if a.mask == "key":
                    sp.wait_ge(pool_rows, 2 if not k else 1 if bs[0] == 0 else bs[-1] + 2)
                op = (Kop if a.nk == 4 else Kself) if k else Qop
                back = (kept_k[a.nk] if k else kept_q)
                for b in bs:
                    for row, src, n in ([(first, KPART[first], n) for first, n in RUNS] if k else [(0, 0, len(QPART))]):
                        sp.dma_start(op[row * DH:(row + n) * DH, b * H:(b + 1) * H, :],
                                     back[src * DH:(src + n) * DH, :, b, :]).then_inc(a.placed[j >= a.early], 16)

            def place_parts(a):
                for j in range(a.ahead, len(a.jobs)):
                    store(a, j)
                    if j > a.ahead:
                        place(a, j - 1)
                place(a, len(a.jobs) - 1)

            def place_max(a, u, par, half):
                sp.wait_ge(a.max_row, u + 1)
                for g in range(4):
                    dst = Qop[ROW_MAX:ROW_MAX + 1, bass.ds(u * HU, HU), :].rearrange(
                        "o h (q g j) -> o (h q) g j", q=QT, g=4)[:, :, g, :]
                    sp.dma_start(dst, mtr[32 * g:32 * g + HU * QT, par, :]).then_inc(a.max_placed[par], 16)

            def mask_rows(row, a):
                for b in range(B):
                    sp.dma_start(Kop[ROW_MASK:ROW_MASK + 1, b * H:(b + 1) * H, :],
                                 row[:, b * SK:(b + 1) * SK].unsqueeze(1).to_broadcast([1, H, SK])).then_inc(a.maskrow_placed, 16)

            def attention(a):
                place_parts(a)
                if a.mask == "key":
                    sp.wait_ge(pool_rows, B + 1)
                    for half in range(2):
                        sp.dma_start(Kop[ROW_MAX:ROW_MAX + 1, half * 32:(half + 1) * 32, :].rearrange("o a k -> o (a k)").bitcast(F32),
                                     I["minus_ones"]).then_inc(a.maskrow_placed, 16)
                    sp.wait_ge(maskrow_ready, 1)
                    mask_rows(maskrow, a)
                place_max(a, 0, 0, 0)
                place_max(a, 1, 1, 0)
                with sp.Fori(1, UNITS // 2) as k:
                    place_max(a, 2 * k, 0, k)
                    place_max(a, 2 * k + 1, 1, k)

            def experts(i, m):
                def load(e, slot, name):
                    w = m.ft * P
                    one = slice(e, e + 1) if isinstance(e, int) else bass.ds(e, 1)
                    sp.dma_start(w1s[:, slot, 0:w + m.ft], I[f"w1{i}"][one, :, :].rearrange("e p f -> p (e f)")).then_inc(m.w_loaded[slot], 16)
                    sp.dma_start(w2s[:, slot, 0:w], I[f"w2{i}"][one, :, :].rearrange("e p f -> p (e f)")).then_inc(m.w_loaded[slot], 16)
                load(0, 0, "")
                load(1, 1, "")
                if i == 0:
                    for e in range(2, E):
                        sp.wait_ge(m.down_ps, (e - 1) * NT)
                        load(e, e % 2, "")
                        if e - 2 < A[2].ahead:
                            store(A[2], e - 2)
                        if 0 <= e - 3 < A[2].ahead:
                            place(A[2], e - 3)
                    return
                with sp.Fori(1, E // 2) as k:
                    sp.wait_ge(m.down_ps, (2 * k - 1) * NT)
                    load(2 * k, 0, "")
                    sp.wait_ge(m.down_ps, 2 * k * NT)
                    load(2 * k + 1, 1, "")

            for i in (1, 2):
                load_weights(i, A[i])
            sp.dma_start(affcol[:], I["affcol"]).then_inc(affine_loaded, 16)
            for i in range(4):
                sp.dma_start(affine[i][:], bcast(I[f"affine{i}"], P)).then_inc(affine_loaded, 16)
            for i, m in enumerate(M):
                sp.dma_start(gateW[i][:], I[f"gateW{i}"]).then_inc(m.small_loaded, 16)
                sp.dma_start(gateB[i][:], bcast(I[f"gateB{i}"], P)).then_inc(m.small_loaded, 16)
                sp.dma_start(b2s[i][:], I[f"b2{i}"]).then_inc(m.small_loaded, 16)
            attention(A[0])
            sp.wait_ge(A[0].pv_done, UNITS)
            sp.dma_start(mkq_raw, I["mask1_kq"]).then_inc(mask1_loaded, 16)
            sp.wait_ge(zerorow_ready, 1)
            mask_rows(zrow, A[1])
            attention(A[1])
            sp.wait_ge(A[1].pv_done, UNITS)
            experts(0, M[0])
            sp.wait_ge(M[0].down_ps, E * NT)
            attention(A[2])
            sp.wait_ge(A[2].pv_done, UNITS)
            experts(1, M[1])
            sp.wait_ge(M[1].down_done, E * NT)
            sp.dma_start(out.rearrange("(t p) d -> p t d", p=P), XB[:]).then_inc(stored, 16)
            sp.wait_ge(stored, 16)

        @block.gpsimd
        def _(pool):
            for b in range(B):
                nc.gpsimd.memset(Kop[:, b * H:(b + 1) * H, :].bitcast(F32), 0.0).then_inc(pool_rows, 1)
                if b == 0:
                    nc.gpsimd.memset(Qop[:].bitcast(F32), ONES_PAIR).then_inc(pool_rows, 1)
            nc.gpsimd.memset(Vcur[:], 0.0)
            nc.gpsimd.memset(mst[:], 0.0)
            nc.gpsimd.memset(eps6[:], 1e-6)
            nc.gpsimd.memset(zrow, 0.0).then_inc(zerorow_ready, 1)
            for e in range(E):
                nc.gpsimd.memset(iota[:, e:e + 1], float(e))
            nc.gpsimd.memset(Vall[:], 1.0).then_inc(pool_const, 1)
            pool.wait_ge(mask1_loaded, 16)
            nc.gpsimd.tensor_scalar(mqk[:], mraw, MASKED, None,
                                    ALU.mult).then_inc(mqk_ready, 1)

            def stage(a, u, par, first=False):
                if not first:
                    pool.wait_ge(a.pv_done, u - 1)
                src = Vall[:, bass.ds(u * HU, HU), 0:a.nk, :].rearrange("p h k d -> p k h d")
                last = nc.gpsimd.tensor_copy(Vcur[:, par, 0:a.nk, :, 0:DH + 1], src)
                last.then_inc(a.vcur_ready, 1)

            def stage_mask(a, u, par, first=False):
                if a.mask == "full":
                    if not first:
                        pool.wait_ge(a.max_row, u - 1)
                    nc.gpsimd.tensor_copy(mcur[:, par, :, :], mqk[:, bass.ds(u // UPB * QT, QT), :]).then_inc(a.mcur_ready, 1)

            for i, a in enumerate(A):
                if i == 1:
                    pool.wait_ge(mask1_loaded, 32)
                    nc.gpsimd.tensor_scalar(mkq[:], mkq_raw, MASKED, None, ALU.mult).then_inc(mkq_ready, 1)
                for j in range(a.ahead):
                    slot = slots[j % RING]
                    pool.wait_ge(a.full_ready, j + 1)
                    if j % RING == 2:
                        pool.wait_ge(N[2].done, N[2].tile0 + NT + 1)
                    if j >= RING:
                        pool.wait_ge(a.kept[j % RING], kept_total(a, j - RING))
                    nc.gpsimd.tensor_copy(slot[:, 0, :], kfull[j]).then_inc(a.hi_ready, 1)
                    pool.wait_ge(a.hi_ready, j + 1)
                    nc.gpsimd.tensor_tensor(krest, kfull[j], slot[:, 0, :], ALU.subtract).then_inc(a.rest_ready, 1)
                    pool.wait_ge(a.rest_ready, j + 1)
                    nc.gpsimd.tensor_copy(slot[:, 1, :], krest).then_inc(a.mid_ready, 1)
                    pool.wait_ge(a.mid_ready, j + 1)
                    nc.gpsimd.tensor_tensor(slot[:, 2, :], krest, slot[:, 1, :], ALU.subtract).then_inc(a.parts_ready, 1)
                    pool.wait_ge(a.parts_ready, j + 1)
                if a.mask == "key":
                    pool.wait_ge(dve_const, 1)
                    for t in range(a.vt):
                        b, k = divmod(t, a.nk)
                        pool.wait_ge(a.v_ready, t + 1)
                        v = Vall[:, b * H:(b + 1) * H, k, :]
                        nc.gpsimd.tensor_scalar(v, v, keep[:, t:t + 1], None, ALU.mult).then_inc(a.v_masked, 1)
                    pool.wait_ge(a.v_masked, a.vt)
                else:
                    pool.wait_ge(a.v_ready, a.vt)
                stage_mask(a, 0, 0, True)
                stage_mask(a, 1, 1, True)
                stage(a, 0, 0, True)
                stage(a, 1, 1, True)
                stage_mask(a, 2, 0)
                stage_mask(a, 3, 1)
                stage_mask(a, 4, 0)
                stage_mask(a, 5, 1)
                with pool.Fori(1, UNITS // 2 - 2) as k:
                    stage(a, 2 * k, 0)
                    stage_mask(a, 2 * k + 4, 0)
                    stage(a, 2 * k + 1, 1)
                    stage_mask(a, 2 * k + 5, 1)
                stage(a, UNITS - 4, 0)
                stage(a, UNITS - 3, 1)
                stage(a, UNITS - 2, 0)
                stage(a, UNITS - 1, 1)
                if a.mask == "key":
                    pool.wait_ge(a.vcur_ready, UNITS)
                    nc.gpsimd.memset(Vall[:], 1.0).then_inc(pool_const, 1)

        @block.scalar
        def _(act):
            def norm_sd(n):
                act.wait_ge(n.var_ready, n.i + 1)
                nc.scalar.activation(sd[:], veps[:], ACT.Sqrt).then_inc(n.sd_ready, 1)

            def norm_transposed(n):
                for half in range(2):
                    act.wait_ge(n.t_ps, n.half0 + half + 1)
                    nc.scalar.copy(xT[:, half * CH:(half + 1) * CH], PS[:, 6 + half, :]).then_inc(n.t_ready, 1)

            def prepare(a):
                nj = len(a.jobs)
                if a.qk_norm:
                    act.wait_ge(pool_const, 1)
                    for j in range(nj):
                        act.wait_ge(a.cent_ready, j + 1)
                        nc.scalar.copy(cbuf[:, j, :], PS[:, j, :])
                        nc.scalar.activation(ubuf[:, j, :], PS[:, j, :], ACT.Square).then_inc(a.sq_ready, 1)
                    for j in range(nj):
                        act.wait_ge(a.var_ready, j + 1)
                        nc.scalar.activation(head_sd[:, j, :], PS[:, j, 0:CH // DH], ACT.Sqrt, bias=eps6[:]).then_inc(a.sd_ready, 1)
                    for j in range(nj):
                        act.wait_ge(a.rs_ready, j + 1)
                        nc.scalar.copy(ubuf[:, j, :].rearrange("p (t d h) -> p t d h", d=DH, h=H),
                                       head_rs[:, j, :].rearrange("p (t h) -> p t h", h=H).unsqueeze(2).to_broadcast(
                                           [P, CH // P, DH, H])).then_inc(a.spread, 1)
                for j in range(a.ahead, nj):
                    r = j % RING
                    act.wait_ge(a.full_ready, j + 1)
                    if j >= RING:
                        act.wait_ge(a.kept[r], kept_total(a, j - RING))
                    nc.scalar.copy(slots[r][:, 0, :], ubuf[:, j, :]).then_inc(a.hi_ready, 1)
                    act.wait_ge(a.rest_ready, j + 1)
                    nc.scalar.copy(slots[r][:, 1, :], rbuf[:, j % 2, :]).then_inc(a.mid_ready, 1)

            def exps(a, u, par, first=False):
                if not first:
                    act.wait_ge(a.pv_done, u - 1)
                for s in range(2 * a.nk):
                    act.wait_ge(a.st_ps, u * 2 * a.nk + s + 1)
                    nc.scalar.activation(prob[:, par, s * CH:(s + 1) * CH], PS[:, 4 + s % 2, :],
                                         ACT.Exp).then_inc(a.exp_done, 1)

            def evacuate(a, u, par, first=False):
                act.wait_ge(a.pv_done, u + 1)
                if not first:
                    act.wait_ge(a.ot_ps, u - 1)
                nc.scalar.copy(osb[:, par, :], PS[:, 6, 0:SQ]).then_inc(a.o_ready, 1)

            def attention(i, a):
                exps(a, 0, 0, True)
                exps(a, 1, 1, True)
                evacuate(a, 0, 0, True)
                exps(a, 2, 0)
                evacuate(a, 1, 1, True)
                with act.Fori(1, UNITS // 2 - 1) as k:
                    exps(a, 2 * k + 1, 1)
                    evacuate(a, 2 * k, 0)
                    exps(a, 2 * k + 2, 0)
                    evacuate(a, 2 * k + 1, 1)
                exps(a, UNITS - 1, 1)
                evacuate(a, UNITS - 2, 0)
                evacuate(a, UNITS - 1, 1)
                for half in range(2):
                    act.wait_ge(a.att_ps, half + 1)
                    nc.scalar.mul(xT[:, half * CH:(half + 1) * CH], PS[:, half, :],
                                  ISQ if i == 2 else 1.0).then_inc(a.att_ready, 1)

            def gates(m):
                act.wait_ge(m.gates.shifted, m.i + 1)
                nc.scalar.activation(gl[1][:], gl[0][:], ACT.Exp).then_inc(m.gates.gate_exp, 1)

            def experts(i, m):
                def hidden(e, j, n0):
                    c = j % 2
                    if n0 is not None:
                        act.wait_ge(m.down_ps, n0)
                    for f in range(m.ft):
                        act.wait_ge(m.up_ps, (e * 2 + c) * m.ft + f + 1)
                        bank = (j * m.ft + f) % 4
                        nc.scalar.activation(hid[:, c, f, :], PS[:, bank, :], m.act,
                                             bias=w1s[:, j // 2, m.ft * P + f:m.ft * P + f + 1]).then_inc(m.hid_ready, 1)
                hidden(0, 0, None)
                hidden(0, 1, None)
                act.wait_ge(m.gates.wt_ps, m.i + 1)
                nc.scalar.copy(wT[:].rearrange("e (a c) -> e a c", a=2), PS[0:E, 4:6, :]).then_inc(m.gates.wt_ready, 1)
                hidden(1, 2, 4)
                hidden(1, 3, 8)
                with act.Fori(1, E // 2) as k:
                    for j in range(4):
                        hidden(2 * k + j // 2, j, k * 16 + 4 * (j - 1))

            act.wait_ge(const_loaded, 16 * 4)
            nc.scalar.copy(identb[:], ident[:]).then_inc(identb_ready, 1)
            norm_sd(N[0])
            norm_transposed(N[0])
            prepare(A[0])
            attention(0, A[0])
            norm_sd(N[1])
            norm_transposed(N[1])
            prepare(A[1])
            attention(1, A[1])
            norm_sd(N[2])
            act.wait_ge(A[2].w_loaded, 16 * 8)
            for j in range(A[2].ahead):
                act.wait_ge(A[2].proj_ready, j + 1)
                nc.scalar.activation(kfull[j], PS[:, j, :], ACT.Identity, bias=W["bk2"][:]).then_inc(A[2].full_ready, 1)
            gates(M[0])
            experts(0, M[0])
            norm_sd(N[3])
            norm_sd(N[4])
            norm_transposed(N[4])
            prepare(A[2])
            attention(2, A[2])
            norm_sd(N[5])
            norm_transposed(N[5])
            gates(M[1])
            experts(1, M[1])

        @block.vector
        def _(dve):
            steps = [0]

            def link(ins):
                steps[0] += 1
                ins.then_inc(dve_step, 1)
                dve.wait_ge(dve_step, steps[0])

            def count(ins):
                steps[0] += 1
                ins.then_inc(dve_step, 1)

            def sync():
                dve.wait_ge(dve_step, steps[0])

            V = nc.vector

            def over_tiles(t):
                return t[:].unsqueeze(1).to_broadcast([P, NT, D])

            def norm(n, src, dst, transposed=True):
                for t in range(NT):
                    count(V.bn_stats(stats[:, t, :], src[:, t, :]))
                sync()
                for t in range(NT):
                    count(V.bn_aggr(mv[:, t, :], stats[:, t, :]))
                sync()
                V.tensor_scalar(veps[:], mv[:, :, 1], 1e-5, None, ALU.add).then_inc(n.var_ready, 1)
                dve.wait_ge(n.sd_ready, n.i + 1)
                link(V.reciprocal(rs[:], sd[:]))
                for t in range(NT):
                    V.tensor_scalar(dst[:, t, :], src[:, t, :], mv[:, t, 0:1], rs[:, t:t + 1],
                                    ALU.subtract, ALU.mult).then_inc(n.done, 1)
                dve.wait_ge(n.done, n.tile0 + NT)

            def prepare(i, a):
                nj = len(a.jobs)
                dve.wait_ge(a.w_loaded, 16 * 8)
                for j, (kind, c) in list(enumerate(a.jobs))[a.ahead:]:
                    dve.wait_ge(a.proj_ready, j + 1)
                    scale = ISQ if (kind == "q" and i == 1) else 1.0
                    ins = V.tensor_scalar(ubuf[:, j, :], PS[:, j, :], W[f"b{kind}{i}"][:], scale,
                                          ALU.add, ALU.mult)
                    ins.then_inc(a.u_ready if a.qk_norm else a.full_ready, 1)
                    if j > a.ahead and not a.qk_norm:
                        split(a, j - 1)
                if a.qk_norm:
                    values(i, a)
                    for j in range(nj):
                        dve.wait_ge(a.sd_ready, j + 1)
                        V.reciprocal(head_rs[:, j, :], head_sd[:, j, :]).then_inc(a.rs_ready, 1)
                    for j, (kind, c) in enumerate(a.jobs):
                        dve.wait_ge(a.rs_ps, j + 1)
                        link(V.tensor_tensor(cbuf[:, j, :], cbuf[:, j, :], PS[:, j, :], ALU.mult))
                        o = 0 if kind == "q" else 2
                        V.tensor_scalar(ubuf[:, j, :], cbuf[:, j, :], lnw[:, o:o + 1],
                                        lnw[:, o + 1:o + 2], ALU.mult, ALU.add).then_inc(a.full_ready, 1)
                        if j:
                            split(a, j - 1)
                split(a, nj - 1)
                if not a.qk_norm:
                    values(i, a)

            def split(a, j):
                dve.wait_ge(a.hi_ready, j + 1)
                V.tensor_tensor(rbuf[:, j % 2, :], ubuf[:, j, :], slots[j % RING][:, 0, :],
                                ALU.subtract).then_inc(a.rest_ready, 1)
                dve.wait_ge(a.mid_ready, j + 1)
                V.tensor_tensor(slots[j % RING][:, 2, :], rbuf[:, j % 2, :], slots[j % RING][:, 1, :],
                                ALU.subtract).then_inc(a.parts_ready, 1)

            def values(i, a):
                if i == 0:
                    dve.wait_ge(pool_const, 1)
                if i == 1:
                    dve.wait_ge(pool_const, 2)
                for t in range(a.vt):
                    b, k = divmod(t, a.nk)
                    if t % 4 == 0:
                        dve.wait_ge(a.v_ps, t // 4 + 1)
                    V.tensor_tensor(Vall[:, b * H:(b + 1) * H, k, 0:DH],
                                    PS[:, 6 + t // 4 % 2, t % 4 * D:(t % 4 + 1) * D].rearrange("p (h d) -> p h d", d=DH),
                                    W[f"bv{i}"][:].rearrange("p (h d) -> p h d", d=DH), ALU.add).then_inc(a.v_ready, 1)

            def maxima(a, u, par, first=False, finish=False):
                if not first:
                    dve.wait_ge(a.max_row, u - 1)
                if a.mask == "full":
                    dve.wait_ge(a.mcur_ready, u + 1)
                    dve.wait_ge(mqk_ready, 1)
                    for s in range(2 * a.nk):
                        if finish and s == a.nk:
                            normalise(a, u - LEAD - 2, 1 - par)
                        if s % 2 == 0:
                            dve.wait_ge(a.max_ps, u * 2 * a.nk + s + 2)
                            V.memset(gate[:, par, s // 2:s // 2 + 1], 0.0)
                        V.tensor_tensor_reduce(out=junk[:, s % 4, :], in0=PS[:, s % 4, :], in1=mcur[:, par, s % 2, :],
                                               scale=1.0, scalar=LOWEST, op0=ALU.add, op1=ALU.max,
                                               accum_out=mstf[:, par, s:s + 1]).then_inc(
                                                   a.max_done if s % 2 else a.max_half, 1)
                    dve.wait_ge(a.max_done, (u + 1) * a.nk)
                    V.tensor_copy(mst[:, par, 0:2 * a.nk], mstf[:, par, 0:2 * a.nk]).then_inc(a.max_col, 1)
                    dve.wait_ge(a.max_col, u + 1)
                else:
                    for p in range(a.nk):
                        if finish and p == a.nk // 2:
                            normalise(a, u - LEAD - 2, 1 - par)
                        dve.wait_ge(a.max_ps, u * 2 * a.nk + 2 * p + 2)
                        banks = PS[:, p % 2 * 2:p % 2 * 2 + 2, :]
                        if a.nk == 4:
                            V.tensor_reduce(mst[:, par, 2 * p:2 * p + 2], banks, AX.X, ALU.max).then_inc(a.max_done, 1)
                        else:
                            V.tensor_reduce(mst[:, par, 4 * p:4 * p + 4].rearrange("p (i q) -> p q i", q=2),
                                            banks.rearrange("p q (i k) -> p q i k", i=2), AX.X,
                                            ALU.max).then_inc(a.max_done, 1)
                    dve.wait_ge(a.max_done, (u + 1) * a.nk)
                if not first:
                    dve.wait_ge(a.max_placed[par], (u - par) * 32)
                V.transpose(mtr[:, par, :], mst[:, par, :]).then_inc(a.max_row, 1)

            def normalise(a, u, par, first=False):
                dve.wait_ge(a.ot_ps, u + 1)
                o = PS[:, 7, :].rearrange("p (r q h c) -> p r q h c", r=2, q=QT, h=HU)[:, 0]
                rd = rden[:, par, :].rearrange("p (q h) -> p q h", q=QT)
                V.reciprocal(rd, o[:, :, :, DH]).then_inc(a.rd_ready, 1)
                dve.wait_ge(a.rd_ready, u + 1)
                dst = att[:, bass.ds(u // UPB, 1), :, bass.ds(u % UPB * HU * DH, HU * DH)].rearrange(
                    "p b q (h d) -> p (b q) h d", h=HU)
                V.tensor_tensor(dst, o[:, :, :, 0:DH],
                                rd.unsqueeze(3).to_broadcast([P, QT, HU, DH]), ALU.mult).then_inc(a.norm_done, 1)

            def attention(i, a):
                if a.mask == "full":
                    for j in range(len(a.jobs) - RING, len(a.jobs)):
                        dve.wait_ge(a.kept[j % RING], kept_total(a, j))
                maxima(a, 0, 0, True)
                maxima(a, 1, 1, True)
                maxima(a, 2, 0)
                maxima(a, 3, 1)
                maxima(a, 4, 0)
                if i == 0:
                    dve.wait_ge(mqk_ready, 1)
                maxima(a, 5, 1, finish=True)
                with dve.Fori(1, UNITS // 2 - 2) as k:
                    maxima(a, 2 * k + 4, 0, finish=True)
                    maxima(a, 2 * k + 5, 1, finish=True)
                for u in range(UNITS - LEAD - 2, UNITS):
                    normalise(a, u, u % 2)

            def project_out(i, a, res, dst):
                for t in range(NT):
                    dve.wait_ge(a.out_ps, t // 4 + 1)
                    V.tensor_tensor(dst[:, t, :], PS[:, 2 + t // 4, t % 4 * D:(t % 4 + 1) * D], res[:, t, :],
                                    ALU.add).then_inc(a.out_done, 1)
                dve.wait_ge(a.out_done, NT)

            def gates(i, m, res):
                g0, g1, g2, g3 = (g[:] for g in gl)
                dve.wait_ge(m.small_loaded, 16 * 3)
                dve.wait_ge(m.gates.logit_ps, m.i + 1)
                gb = gateB[i][:].unsqueeze(1).to_broadcast([P, NT, E])
                link(V.tensor_tensor(g2, PS[:, 7, 0:NT * E].rearrange("p (t e) -> p t e", e=E), gb, ALU.add))
                link(V.tensor_reduce(gs[:], g2, AX.X, ALU.max))
                per = gs[:].unsqueeze(2).to_broadcast([P, NT, E])
                V.tensor_tensor(g0, g2, per, ALU.subtract).then_inc(m.gates.shifted, 1)
                dve.wait_ge(m.gates.gate_exp, m.i + 1)
                link(V.tensor_reduce(gs[:], g1, AX.X, ALU.add))
                link(V.reciprocal(rs[:], gs[:]))
                link(V.tensor_tensor(g2, g1, rs[:].unsqueeze(2).to_broadcast([P, NT, E]), ALU.mult))
                for t in range(NT):
                    count(V.max(g8[:, t, :], gl[2][:, t, :]))
                sync()
                for t in range(NT):
                    count(V.max_index(gi[:, t, :], g8[:, t, :], gl[2][:, t, :]))
                sync()
                link(V.tensor_copy(gif[:], gi[:]))
                io = iota[:].unsqueeze(1).to_broadcast([P, NT, E])
                pick = lambda k: gif[:, :, k:k + 1].to_broadcast([P, NT, E])
                if m.topk == 1:
                    V.tensor_tensor(gw_[:], io, pick(0), ALU.is_equal).then_inc(m.gates.weight_ready, 1)
                else:
                    link(V.tensor_tensor(g3, io, pick(0), ALU.is_equal))
                    link(V.tensor_tensor(g0, io, pick(1), ALU.is_equal))
                    link(V.tensor_tensor(g3, g3, g0, ALU.add))
                    V.tensor_tensor(gw_[:], g3, g2, ALU.mult).then_inc(m.gates.weight_ready, 1)
                dve.wait_ge(m.gates.weight_ready, m.i + 1)
                dve.wait_ge(m.gates.b2_ps, m.i + 1)
                V.tensor_tensor(XB[:], PS[:, 6:8, :].rearrange("p a (t d) -> p (a t) d", d=D), res,
                                ALU.add).then_inc(m.gates.acc_ready, 1)
                dve.wait_ge(m.gates.acc_ready, m.i + 1)

            def experts(i, m):
                def add(e, first=False):
                    for t in range(NT):
                        n = e * NT + t
                        dve.wait_ge(m.down_ps, n + 1)
                        if not first:
                            dve.wait_ge(m.down_done, n + 1 - NT)
                        V.scalar_tensor_tensor(XB[:, t, :], PS[:, 4 + t % 4, 0:D],
                                               gw_[:, t, bass.ds(e, 1)], XB[:, t, :],
                                               ALU.mult, ALU.add).then_inc(m.down_done, 1)
                add(0, True)
                with dve.Fori(1, E) as e:
                    add(e)
                dve.wait_ge(m.down_done, E * NT)

            dve.wait_ge(x_loaded, 16)
            norm(N[0], X, XN)
            dve.wait_ge(masks_loaded, 16 * 2)
            V.tensor_copy(keep[:], keepraw[:]).then_inc(dve_const, 1)
            link(V.tensor_copy(maskrow, maskrow_raw))
            V.tensor_scalar(maskrow, maskrow, 1.0, -MASKED, ALU.subtract, ALU.mult).then_inc(maskrow_ready, 1)
            dve.wait_ge(maskrow_ready, 1)
            dve.wait_ge(const_loaded, 16 * 4)
            link(V.tensor_scalar(lnw[:, 0:2], lnw[:, 0:2], ISQ, None, ALU.mult))
            prepare(0, A[0])
            attention(0, A[0])
            link(V.tensor_tensor(XB[:], X[:], over_tiles(W["bo0"]), ALU.add))
            project_out(0, A[0], XB, X)
            norm(N[1], X, XN)
            dve.wait_ge(A[1].w_loaded, 16 * 8)
            link(V.tensor_tensor(XB[:], XN[:], over_tiles(W["bo1"]), ALU.add))
            prepare(1, A[1])
            attention(1, A[1])
            project_out(1, A[1], XB, XB)
            norm(N[2], XB, XN)
            dve.wait_ge(affine_loaded, 16 * 5)
            for half in range(2):
                dve.wait_ge(N[2].t_ps, N[2].half0 + half + 1)
                V.tensor_scalar(xT[:, half * CH:(half + 1) * CH], PS[:, 6 + half, :], affcol[:, 0:1], affcol[:, 1:2],
                                ALU.mult, ALU.add).then_inc(N[2].t_ready, 1)
            kept = att[:].rearrange("p b q c -> p (b q) c")
            link(V.tensor_tensor(kept, XN[:], over_tiles(affine[0]), ALU.mult))
            V.tensor_tensor(kept, kept, over_tiles(affine[1]), ALU.add).then_inc(N[2].done, 1)
            dve.wait_ge(N[2].done, N[2].tile0 + NT + 1)
            gates(0, M[0], kept)
            experts(0, M[0])
            dve.wait_ge(A[2].kept[2], kept_total(A[2], 2))
            norm(N[3], XB, XN)
            link(V.tensor_tensor(XN[:], XN[:], over_tiles(affine[2]), ALU.mult))
            link(V.tensor_tensor(XN[:], XN[:], over_tiles(affine[3]), ALU.add))
            link(V.tensor_tensor(X[:], X[:], XN[:], ALU.add))
            norm(N[4], X, XN)
            dve.wait_ge(A[2].w_loaded, 16 * 8)
            prepare(2, A[2])
            attention(2, A[2])
            link(V.tensor_tensor(XB[:], X[:], over_tiles(W["bo2"]), ALU.add))
            project_out(2, A[2], XB, X)
            norm(N[5], X, XN)
            gates(1, M[1], X[:])
            experts(1, M[1])

        @block.tensor
        def _(pe):
            mm = nc.tensor.matmul

            def norm_transpose(n):
                pe.wait_ge(const_loaded, 16 * 4)
                for half in range(2):
                    pe.wait_ge(n.done, n.tile0 + 4 * half + 4)
                    for t in range(4 * half, 4 * half + 4):
                        last = nc.tensor.transpose(PS[:, 6 + half, t % 4 * P:(t % 4 + 1) * P], XN[:, t, :], ident[:])
                    last.then_inc(n.t_ps, 1)

            def prepare(i, a, n):
                pe.wait_ge(a.w_loaded, 16 * 8)
                pe.wait_ge(ctx_loaded, 16)
                for j, (kind, c) in list(enumerate(a.jobs))[a.ahead:]:
                    src = xT if kind == "q" else a.src
                    if j == 0 or src is xT:
                        pe.wait_ge(n.t_ready, n.half0 + 2)
                    mm(PS[:, j, :], W[f"{kind}{i}"][:], src[:, c * CH:(c + 1) * CH], start=True, stop=True).then_inc(a.proj_ready, 1)
                if a.qk_norm:
                    for j in range(len(a.jobs)):
                        pe.wait_ge(a.u_ready, j + 1)
                        mm(PS[:, j, :], cmat[:], ubuf[:, j, :], start=True, stop=True).then_inc(a.cent_ready, 1)
                    value_products(i, a)
                    for j in range(len(a.jobs)):
                        pe.wait_ge(a.sq_ready, j + 1)
                        for t in range(CH // P):
                            last = mm(PS[:, j, t * H:(t + 1) * H], ubuf[:, j, t * P:(t + 1) * P], gmat[:],
                                      start=True, stop=True)
                        last.then_inc(a.var_ready, 1)
                    for j in range(len(a.jobs)):
                        pe.wait_ge(a.spread, j + 1)
                        for t in range(CH // P):
                            last = nc.tensor.transpose(PS[:, j, t * P:(t + 1) * P], ubuf[:, j, t * P:(t + 1) * P], ident[:])
                        last.then_inc(a.rs_ps, 1)
                else:
                    value_products(i, a)

            def value_products(i, a):
                for t in range(a.vt):
                    if t % 4 == 0 and t >= 8:
                        pe.wait_ge(a.v_ready, t - 4)
                    last = mm(PS[:, 6 + t // 4 % 2, t % 4 * D:(t % 4 + 1) * D], a.src[:, t * P:(t + 1) * P],
                              W[f"v{i}"][:], start=True, stop=True)
                    if t % 4 == 3:
                        last.then_inc(a.v_ps, 1)

            def max_slot(a, u, s, first=False):
                n = u * 2 * a.nk + s
                if s % 2 == 0 and not (first and s < 4):
                    pe.wait_ge(a.max_done, u * a.nk + s // 2 - 1)
                bank = s % 4
                hp, q = divmod(s, 2)
                if a.nk == 4:
                    last = mm(PS[:, bank, :], unit_head(Qop, u, hp, ROW_MAX, q * P, P),
                              unit_head(Kop, u, hp, ROW_MAX, 0, SK), start=True, stop=True)
                else:
                    for i in range(2):
                        last = mm(PS[:, bank, i * SQ:(i + 1) * SQ], unit_head(Qop, u, 2 * hp + i, ROW_MAX, q * P, P),
                                  unit_head(Kself, u, 2 * hp + i, ROW_MAX, 0, SQ), start=True, stop=True)
                last.then_inc(a.max_ps, 1)

            def unit_head(op, u, h, rows, first, n):
                return op[0:rows, bass.ds(u * HU + h, 1), first:first + n].rearrange("p o c -> p (o c)")

            def score_slot(a, u, s, first=False):
                n = u * 2 * a.nk + s
                if not (first and s < 2):
                    pe.wait_ge(a.exp_done, n - 1)
                bank = 4 + s % 2
                h, kt0 = divmod(2 * s, a.nk)
                K = Kop if a.nk == 4 else Kself
                if a.mask == "full":
                    mm(PS[:, bank, :], identb[:], mkq[:, bass.ds(u // UPB * 2 + s % 2, 1), :].rearrange("p o k -> p (o k)"),
                       start=True, stop=False, skip_group_check=True)
                for kk in range(2):
                    last = mm(PS[:, bank, kk * SQ:(kk + 1) * SQ],
                              unit_head(K, u, h, KROWS, (kt0 + kk) * P, P), unit_head(Qop, u, h, KROWS, 0, SQ),
                              start=a.mask != "full", stop=True, skip_group_check=True)
                last.then_inc(a.st_ps, 1)

            def value_tile(a, u, par, kt):
                for h in range(HU):
                    last = mm(PS[32 * h:32 * h + 32, 6, 0:SQ], Vcur[:, par, kt, h, :],
                              prob[:, par, (h * a.nk + kt) * SQ:(h * a.nk + kt + 1) * SQ],
                              start=kt == 0, stop=kt == a.nk - 1)
                if kt == a.nk - 1:
                    last.then_inc(a.pv_done, 1)

            def to_tokens(a, u, par, first=False):
                pe.wait_ge(a.o_ready, u + 1)
                if not first:
                    pe.wait_ge(a.norm_done, u)
                for q in range(QT):
                    last = nc.tensor.transpose(PS[:, 7, q * P:(q + 1) * P], osb[:, par, q * P:(q + 1) * P], ident[:])
                last.then_inc(a.ot_ps, 1)

            def step(a, u, par, half, maxes=True, scores=True, values=True, tokens=True, first=False, ftok=False):
                if scores:
                    pe.wait_ge(a.max_placed[par], half * 64 + 64)
                for i in range(a.nk):
                    if tokens and i == a.nk // 2:
                        to_tokens(a, u - 2, par, ftok)
                    for s in (2 * i, 2 * i + 1):
                        if maxes:
                            max_slot(a, u + LEAD, s)
                        if scores:
                            score_slot(a, u, s, first)
                    if values:
                        if i == 0:
                            pe.wait_ge(a.exp_done, u * 2 * a.nk)
                            pe.wait_ge(a.vcur_ready, u)
                            if not first_values(u):
                                pe.wait_ge(a.o_ready, u - 1)
                        value_tile(a, u - 1, 1 - par, i)

            def first_values(u):
                return isinstance(u, int) and u == 1

            def attention(i, a):
                pe.wait_ge(a.placed[0], placed_total(a, False))
                if i < 2:
                    pe.wait_ge(a.maskrow_placed, 16 * (B + 2 * (i == 0)))
                pe.wait_ge(a.v_ready, a.vt)
                if i == 1:
                    pe.wait_ge(mkq_ready, 1)
                for u in range(LEAD):
                    for s in range(2 * a.nk):
                        max_slot(a, u, s, first=u == 0)
                step(a, 0, 0, 0, values=False, tokens=False, first=True)
                step(a, 1, 1, 0, tokens=False)
                step(a, 2, 0, 1, ftok=True)
                pe.wait_ge(a.placed[1], placed_total(a, True))
                with pe.Fori(1, UNITS // 2 - 2) as k:
                    step(a, 2 * k + 1, 1, k)
                    step(a, 2 * k + 2, 0, k + 1)
                step(a, UNITS - 3, 1, UNITS // 2 - 2, maxes=False)
                step(a, UNITS - 2, 0, UNITS // 2 - 1, maxes=False)
                step(a, UNITS - 1, 1, UNITS // 2 - 1, maxes=False)
                step(a, UNITS, 0, 0, maxes=False, scores=False)
                to_tokens(a, UNITS - 1, 1)
                pe.wait_ge(a.norm_done, UNITS)
                for half in range(2):
                    for t in range(4 * half, 4 * half + 4):
                        last = nc.tensor.transpose(PS[:, half, t % 4 * P:(t % 4 + 1) * P], att[:, t // QT, t % QT, :], ident[:])
                    last.then_inc(a.att_ps, 1)
                for t in range(NT):
                    if t % 4 == 0:
                        pe.wait_ge(a.att_ready, t // 4 + 1)
                    last = mm(PS[:, 2 + t // 4, t % 4 * D:(t % 4 + 1) * D], xT[:, t * P:(t + 1) * P], W[f"o{i}"][:],
                       start=True, stop=True)
                    if t % 4 == 3:
                        last.then_inc(a.out_ps, 1)

            def logits(i, m, n):
                pe.wait_ge(m.small_loaded, 16 * 3)
                pe.wait_ge(n.t_ready, n.half0 + 2)
                for t in range(NT):
                    last = mm(PS[:, 7, t * E:(t + 1) * E], xT[:, t * P:(t + 1) * P], gateW[i][:], start=True, stop=True)
                last.then_inc(m.gates.logit_ps, 1)

            def weighted_biases(i, m):
                pe.wait_ge(m.gates.weight_ready, m.i + 1)
                for t in range(NT):
                    last = nc.tensor.transpose(PS[0:E, 4 + t // 4, t % 4 * P:(t % 4 + 1) * P], gw_[:, t, :], ident[:])
                last.then_inc(m.gates.wt_ps, 1)
                pe.wait_ge(m.gates.wt_ready, m.i + 1)
                for t in range(NT):
                    last = mm(PS[:, 6 + t // 4, t % 4 * D:(t % 4 + 1) * D], wT[:, t * P:(t + 1) * P], b2s[i][:], start=True, stop=True)
                last.then_inc(m.gates.b2_ps, 1)
                pe.wait_ge(m.gates.acc_ready, m.i + 1)

            def experts(i, m):
                def up(e, j, first=False):
                    c = j % 2
                    if c == 0:
                        pe.wait_ge(m.w_loaded[j // 2], (e - j // 2) * 16 + 32)
                    for f in range(m.ft):
                        n = (e * 2 + c) * m.ft + f
                        if not (first and c * m.ft + f < 4):
                            pe.wait_ge(m.hid_ready, n - 3)
                        mm(PS[:, (j * m.ft + f) % 4, :], w1s[:, j // 2, f * P:(f + 1) * P],
                           xT[:, c * CH:(c + 1) * CH], start=True, stop=True).then_inc(m.up_ps, 1)

                def down(e, j, first=False):
                    c = j % 2
                    pe.wait_ge(m.hid_ready, (e * 2 + c + 1) * m.ft)
                    for t in range(4):
                        n = e * NT + 4 * c + t
                        if not (first and c == 0):
                            pe.wait_ge(m.down_done, n - 3)
                        for f in range(m.ft):
                            last = mm(PS[:, 4 + t, 0:D], hid[:, c, f, t * P:(t + 1) * P],
                                      w2s[:, j // 2, f * D:(f + 1) * D], start=f == 0, stop=f == m.ft - 1)
                        last.then_inc(m.down_ps, 1)

                up(0, 0, True)
                up(0, 1, True)
                weighted_biases(i, m)
                down(0, 0, True)
                up(1, 2)
                down(0, 1)
                up(1, 3)
                down(1, 2)
                with pe.Fori(1, E // 2) as k:
                    up(2 * k, 0)
                    down(2 * k - 1, 3)
                    up(2 * k, 1)
                    down(2 * k, 0)
                    up(2 * k + 1, 2)
                    down(2 * k, 1)
                    up(2 * k + 1, 3)
                    down(2 * k + 1, 2)
                down(E - 1, 3)

            norm_transpose(N[0])
            pe.wait_ge(identb_ready, 1)
            prepare(0, A[0], N[0])
            attention(0, A[0])
            norm_transpose(N[1])
            prepare(1, A[1], N[1])
            attention(1, A[1])
            pe.wait_ge(A[2].w_loaded, 16 * 8)
            pe.wait_ge(A[1].out_done, NT)
            for j in range(A[2].ahead):
                mm(PS[:, j, :], W["k2"][:], ctxT[:, j * CH:(j + 1) * CH], start=True, stop=True).then_inc(A[2].proj_ready, 1)
            norm_transpose(N[2])
            pe.wait_ge(A[2].full_ready, A[2].ahead)
            logits(0, M[0], N[2])
            experts(0, M[0])
            norm_transpose(N[4])
            prepare(2, A[2], N[4])
            attention(2, A[2])
            norm_transpose(N[5])
            logits(1, M[1], N[5])
            experts(1, M[1])


def kernel(**inputs):
    import numpy as np
    import concourse.bacc as bacc
    from concourse.bass_utils import run_bass_kernel_spmd

    g = {k: np.asarray(v) for k, v in inputs.items()}
    rows = lambda a: np.ascontiguousarray(a)
    col = lambda a: rows(a.reshape(P, 1))
    heads = lambda a: np.repeat(a, H)
    by_dim = lambda a: rows(a.reshape(-1, H, DH).transpose(0, 2, 1).reshape(-1, D))
    centre = np.kron(np.eye(DH) - np.full((DH, DH), 1.0 / DH), np.eye(H)).astype(np.float32)
    mean = np.kron(np.full((DH, 1), 1.0 / DH), np.eye(H)).astype(np.float32)
    m1 = g["mask_BxSxS2_bk1"]
    m0 = g["mask_BxS2_bk0"]
    x0, xf, x1, f1 = "L0_xattn_", "L0_ffn_", "L1_xattn_", "L1_ffn_"
    Wkv, bkv = g[x0 + "Wkv"], g[x0 + "bkv"]

    def up(w, b, ft):
        return rows(np.concatenate([w, b.reshape(E, ft, P).transpose(0, 2, 1)], 2))

    def down(w, ft):
        return rows(w.reshape(E, ft, P, D).transpose(0, 2, 1, 3).reshape(E, P, ft * D))

    a = {
        "x": rows(g["x"].reshape(TOK, D)),
        "ctxT": rows(g["ctx_1024"].reshape(B * SK, D).T),
        "mask0_row": rows(m0.reshape(1, B * SK)),
        "mask0_col": rows(m0.reshape(B * SK // P, P).T),
        "mask1_qk": rows(m1.reshape(B * QT, P, SK).transpose(1, 0, 2)),
        "mask1_kq": rows(m1.reshape(B, SQ, SK // P, P).transpose(3, 0, 2, 1).reshape(P, B * 2, 2 * SQ)),
        "minus_ones": np.full((1, B * H * SK // 4), MINUS_ONES_PAIR, np.float32),
        "ident": np.eye(P, dtype=np.float32), "cmat": centre, "gmat": mean,
        "lnw": rows(np.stack([heads(g[x0 + n]) for n in ("qn_w", "qn_b", "kn_w", "kn_b")], 1)),
        "wq0": by_dim(g[x0 + "Wq"].T), "wk0": by_dim(Wkv[:D].T), "wv0": rows(Wkv[D:].T), "wo0": rows(g[x0 + "Wo"].T),
        "bq0": col(by_dim(g[x0 + "bq"])), "bk0": col(by_dim(bkv[:D])), "bv0": rows(bkv[D:]), "bo0": g[x0 + "bo"],
        "wq1": by_dim(g[xf + "Wq"]), "wk1": by_dim(g[xf + "Wk"]), "wv1": g[xf + "Wv"], "wo1": g[xf + "Wo"],
        "bq1": col(by_dim(g[xf + "bq"])), "bk1": col(by_dim(g[xf + "bk"])), "bv1": g[xf + "bv"], "bo1": g[xf + "bo"],
        "wq2": by_dim(g[x1 + "Wq"].reshape(D, D)), "wk2": by_dim(g[x1 + "Wk"].reshape(D, D)),
        "wv2": rows(g[x1 + "Wv"].reshape(D, D)), "wo2": rows(g[x1 + "Wo"].reshape(D, D)),
        "bq2": col(by_dim(g[x1 + "bq"])), "bk2": col(by_dim(g[x1 + "bk"])), "bv2": rows(g[x1 + "bv"].reshape(D)), "bo2": g[x1 + "bo"],
        "affcol": rows(np.stack([g[xf + "ln1_g"], g[xf + "ln1_b"]], 1)),
        "affine0": g[xf + "ln1_g"], "affine1": g[xf + "ln1_b"], "affine2": g[xf + "ln2_g"], "affine3": g[xf + "ln2_b"],
        "gateW0": g[xf + "gW"], "gateB0": g[xf + "gb"], "b20": g[xf + "b2"],
        "w10": up(g[xf + "W1"], g[xf + "b1"], 2), "w20": down(g[xf + "W2"], 2),
        "gateW1": g[f1 + "w_router"], "gateB1": g[f1 + "b_router"], "b21": g[f1 + "b2"],
        "w11": up(g[f1 + "w1"], g[f1 + "b1"], 4), "w21": down(g[f1 + "w2"], 4),
    }
    nc = bacc.Bacc("TRN2", target_bir_lowering=False, num_devices=1, dynamic_dma_scratch_size=1024)
    aps = {n: nc.dram_tensor("in_" + n, v.shape, mybir.dt.from_np(v.dtype), kind="ExternalInput").ap()
           for n, v in a.items()}
    out = nc.dram_tensor("out", (TOK, D), F32, kind="ExternalOutput").ap()
    build(nc, aps, out)
    r = run_bass_kernel_spmd(nc, [{"in_" + n: v for n, v in a.items()}], core_ids=[0])
    return r.results[0]["out"].reshape(B, SQ, D)
```
